# Optimizing a Trainium2 kernel written in Bass

```python
import numpy as np
import jax
import jax.numpy as jnp

def _softmax(x, axis=-1):
    return jax.nn.softmax(x, axis=axis)

def _gelu(x):
    return jax.nn.gelu(x, approximate=True)

def _silu(x):
    return jax.nn.silu(x)

def _sigmoid(x):
    return jax.nn.sigmoid(x)

def _layernorm(x, axis=-1, eps=1e-05):
    m = jnp.mean(x, axis=axis, keepdims=True)
    v = jnp.var(x, axis=axis, keepdims=True)
    return (x - m) / jnp.sqrt(v + eps)

def _scatter_add(tgt, idx, src, axis=0):
    return tgt.at[idx].add(src)

def _segment_sum(src, seg, n):
    return jax.ops.segment_sum(src, seg, n)
kernel_name = 'mk_adj_resnorm_d1_adj_r2_ab4990'

def setup_inputs(seed: int=0):
    np.random.seed(seed)
    _w = jnp.asarray

    def _rec_inputs():
        import jax
        import jax.numpy as jnp
        _gk = jax.random.key(seed)
        x = 7.22e-05 + 1 * jax.random.normal(jax.random.fold_in(_gk, 1), (16, 512, 128), jnp.float32)
        _w = (1.0 + jnp.arange(512, dtype=jnp.float32)) ** (-0.5)
        _w = _w / _w.mean()
        _pij = jnp.clip(0.03125 * _w[:, None] * _w[None, :], 0.0, 1.0)
        _a = jax.random.uniform(jax.random.fold_in(_gk, 2), (16, 512, 512)) < _pij
        _a = jnp.logical_or(_a, jnp.swapaxes(_a, -1, -2))
        _a = jnp.logical_or(_a, jnp.eye(512, dtype=bool))
        _af = _a.astype(jnp.float32)
        adj = _af
        return (x, adj)
    x, adj = _rec_inputs()

    def _L0_gnn_setup():
        import jax, jax.numpy as jnp
        import numpy as np
        from jax import lax
        DIM = 128
        EPS = 1e-05

        def _bn(h, g, b, m, v):
            scale = g / jnp.sqrt(v + EPS)
            return h * scale[None, :, None] + (b - m * scale)[None, :, None]

        def _conv1d(h, w, pad):
            return lax.conv_general_dilated(h, w, window_strides=(1,), padding=[(pad, pad)], dimension_numbers=('NCH', 'OIH', 'NCH'))
        key = jax.random.key(seed)
        ks = jax.random.split(key, 16)
        bs, n, d = (16, 1024, DIM)
        s = 0.05
        return {'x': jax.random.normal(ks[0], (bs, n, d), jnp.float32), 'mask': jnp.ones((bs, n, n), jnp.float32), 'w_se': jax.random.normal(ks[1], (3, d), jnp.float32) * s, 'b_se': jnp.zeros((3,), jnp.float32), 'conv1_w': jax.random.normal(ks[2], (d, d, 1), jnp.float32) * s, 'bn1_g': jnp.ones((d,), jnp.float32), 'bn1_b': jnp.zeros((d,), jnp.float32), 'bn1_m': jnp.zeros((d,), jnp.float32), 'bn1_v': jnp.ones((d,), jnp.float32), 'conv2_w': jax.random.normal(ks[3], (d, d, 17), jnp.float32) * s, 'bn2_g': jnp.ones((d,), jnp.float32), 'bn2_b': jnp.zeros((d,), jnp.float32), 'bn2_m': jnp.zeros((d,), jnp.float32), 'bn2_v': jnp.ones((d,), jnp.float32), 'w_msg': jax.random.normal(ks[4], (d, d), jnp.float32) * s, 'b_msg': jnp.zeros((d,), jnp.float32), 'w_ih': jax.random.normal(ks[5], (3 * d, 2 * d), jnp.float32) * s, 'b_ih': jnp.zeros((3 * d,), jnp.float32), 'w_hh': jax.random.normal(ks[6], (3 * d, d), jnp.float32) * s, 'b_hh': jnp.zeros((3 * d,), jnp.float32)}
    _L0_gnn_all = _L0_gnn_setup()
    _L0_gnn_in = {k: v for k, v in _L0_gnn_all.items() if k in ('w_se', 'b_se', 'conv1_w', 'bn1_g', 'bn1_b', 'bn1_m', 'bn1_v', 'conv2_w', 'bn2_g', 'bn2_b', 'bn2_m', 'bn2_v', 'w_msg', 'b_msg', 'w_ih', 'b_ih', 'w_hh', 'b_hh')}
    del _L0_gnn_all
    return {'x': x, 'adj': adj, 'L0_gnn_w_se': _L0_gnn_in['w_se'], 'L0_gnn_b_se': _L0_gnn_in['b_se'], 'L0_gnn_conv1_w': _L0_gnn_in['conv1_w'], 'L0_gnn_bn1_g': _L0_gnn_in['bn1_g'], 'L0_gnn_bn1_b': _L0_gnn_in['bn1_b'], 'L0_gnn_bn1_m': _L0_gnn_in['bn1_m'], 'L0_gnn_bn1_v': _L0_gnn_in['bn1_v'], 'L0_gnn_conv2_w': _L0_gnn_in['conv2_w'], 'L0_gnn_bn2_g': _L0_gnn_in['bn2_g'], 'L0_gnn_bn2_b': _L0_gnn_in['bn2_b'], 'L0_gnn_bn2_m': _L0_gnn_in['bn2_m'], 'L0_gnn_bn2_v': _L0_gnn_in['bn2_v'], 'L0_gnn_w_msg': _L0_gnn_in['w_msg'], 'L0_gnn_b_msg': _L0_gnn_in['b_msg'], 'L0_gnn_w_ih': _L0_gnn_in['w_ih'], 'L0_gnn_b_ih': _L0_gnn_in['b_ih'], 'L0_gnn_w_hh': _L0_gnn_in['w_hh'], 'L0_gnn_b_hh': _L0_gnn_in['b_hh']}

def reference(x, adj, L0_gnn_w_se, L0_gnn_b_se, L0_gnn_conv1_w, L0_gnn_bn1_g, L0_gnn_bn1_b, L0_gnn_bn1_m, L0_gnn_bn1_v, L0_gnn_conv2_w, L0_gnn_bn2_g, L0_gnn_bn2_b, L0_gnn_bn2_m, L0_gnn_bn2_v, L0_gnn_w_msg, L0_gnn_b_msg, L0_gnn_w_ih, L0_gnn_b_ih, L0_gnn_w_hh, L0_gnn_b_hh):
    import jax
    import jax.numpy as jnp

    def _L0_gnn_ref(x, mask, w_se, b_se, conv1_w, bn1_g, bn1_b, bn1_m, bn1_v, conv2_w, bn2_g, bn2_b, bn2_m, bn2_v, w_msg, b_msg, w_ih, b_ih, w_hh, b_hh):
        import jax, jax.numpy as jnp
        import numpy as np
        from jax import lax
        DIM = 128
        EPS = 1e-05

        def _bn(h, g, b, m, v):
            scale = g / jnp.sqrt(v + EPS)
            return h * scale[None, :, None] + (b - m * scale)[None, :, None]

        def _conv1d(h, w, pad):
            return lax.conv_general_dilated(h, w, window_strides=(1,), padding=[(pad, pad)], dimension_numbers=('NCH', 'OIH', 'NCH'))
        d = x.shape[-1]
        xc = jnp.transpose(x, (0, 2, 1))
        h = _bn(_conv1d(xc, conv1_w, 0), bn1_g, bn1_b, bn1_m, bn1_v)
        h = jax.nn.relu(h)
        h = _bn(_conv1d(h, conv2_w, 8), bn2_g, bn2_b, bn2_m, bn2_v)
        x_conv = jnp.transpose(jax.nn.relu(h + xc), (0, 2, 1))
        s = x @ w_se.T + b_se
        sq = jnp.sum(s * s, axis=-1)
        dist = sq[:, :, None] + sq[:, None, :] - 2.0 * jnp.einsum('bnd,bmd->bnm', s, s)
        A = jnp.exp(-dist) * mask
        msg = jax.nn.relu(x @ w_msg.T + b_msg)
        x_nmp = jnp.einsum('bnm,bmd->bnd', A, msg)
        x_in = jnp.concatenate([x_conv, x_nmp], axis=-1)
        gi = x_in @ w_ih.T + b_ih
        gh = x @ w_hh.T + b_hh
        gi_r, gi_z, gi_n = (gi[..., :d], gi[..., d:2 * d], gi[..., 2 * d:])
        gh_r, gh_z, gh_n = (gh[..., :d], gh[..., d:2 * d], gh[..., 2 * d:])
        r = jax.nn.sigmoid(gi_r + gh_r)
        z = jax.nn.sigmoid(gi_z + gh_z)
        nn_ = jnp.tanh(gi_n + r * gh_n)
        return (1.0 - z) * nn_ + z * x
    x = _layernorm(x + _L0_gnn_ref(x, adj, L0_gnn_w_se, L0_gnn_b_se, L0_gnn_conv1_w, L0_gnn_bn1_g, L0_gnn_bn1_b, L0_gnn_bn1_m, L0_gnn_bn1_v, L0_gnn_conv2_w, L0_gnn_bn2_g, L0_gnn_bn2_b, L0_gnn_bn2_m, L0_gnn_bn2_v, L0_gnn_w_msg, L0_gnn_b_msg, L0_gnn_w_ih, L0_gnn_b_ih, L0_gnn_w_hh, L0_gnn_b_hh), axis=-1)
    return x

_drawn_inputs = setup_inputs


def setup_inputs(seed=0):
    import zlib

    import numpy as np

    out = dict(_drawn_inputs(seed))
    spreads = {'L0_gnn_b_se': (0.0, 0.8),
     'L0_gnn_bn1_g': (1.0, 0.6),
     'L0_gnn_bn1_b': (0.0, 0.538),
     'L0_gnn_bn1_m': (0.0, 0.48),
     'L0_gnn_bn1_v': (1.0, 0.6),
     'L0_gnn_bn2_g': (1.0, 0.6),
     'L0_gnn_bn2_b': (0.0, 0.8),
     'L0_gnn_bn2_m': (0.0, 0.76),
     'L0_gnn_bn2_v': (1.0, 0.6),
     'L0_gnn_b_msg': (0.0, 0.1),
     'L0_gnn_b_ih': (0.0, 0.302),
     'L0_gnn_b_hh': (0.0, 0.415)}
    factors = {}
    for name, (base, spread) in spreads.items():
        noise = np.random.default_rng([zlib.crc32(name.encode()), seed]).standard_normal(out[name].shape)
        drawn = base * np.exp(spread * noise) if base else spread * noise
        out[name] = jnp.asarray(drawn.astype(out[name].dtype))
    for name, factor in factors.items():
        out[name] = (out[name] * factor).astype(out[name].dtype)
    return out
```

```python
from contextlib import ExitStack

import numpy as np
import concourse.bass as bass
from concourse import mybir

F32 = mybir.dt.float32
F32R = mybir.dt.float32r
ALU = mybir.AluOpType
ACT = mybir.ActivationFunctionType

EPS = 1e-5
P = 128


def gnn_program(nc, ins, out):
    x, adj = ins["x"], ins["adj"]
    w = {name[len("L0_gnn_"):]: ap for name, ap in ins.items() if name.startswith("L0_gnn_")}
    B, N, D = x.shape
    NCH = N // P
    TAPS = w["conv2_w"].shape[2]
    PAD = (TAPS - 1) // 2
    SE = w["w_se"].shape[0]
    assert D == P and N == 512 and B % 2 == 0 and B >= 6 and SE == 3

    MC = D + SE + 1
    NK = 4 * SE + 4
    SQ, ONE = 4 * SE, 4 * SE + 2
    RHS = 32

    W_IH_X, W_IH_NMP, W_HH = 0, 3, 6
    W_CONV1, W_CONV2 = 9, 10
    NW = W_CONV2 + TAPS

    VEC = ["bn1_g", "bn1_b", "bn1_m", "bn1_v", "bn2_g", "bn2_b", "bn2_m", "bn2_v", "b_ih", "b_hh"]
    G1, B1, M1, V1, G2, B2, M2, V2, BIH, BHH, NVEC = 0, 1, 2, 3, 4, 5, 6, 7, 8, 11, 14

    with ExitStack() as ctx:
        def sb(name, shape, dt=F32):
            return ctx.enter_context(nc.sbuf_tensor(name, shape, dt))

        def bank(name, n=1):
            return ctx.enter_context(nc.psum_tensor(name, [P, 512] if n == 1 else [P, n, 512], F32))

        def sem(name):
            return ctx.enter_context(nc.semaphore(name))

        x_nat = sb("x_nat", [P, 2, NCH, D])
        adj_nat = sb("adj_nat", [P, 2, NCH, N])
        vec_rows = sb("vec_rows", [NVEC, P])
        bias_row = sb("bias_row", [1, 2, MC])
        wc1_nat = sb("wc1_nat", [P, D])
        wc2_nat = sb("wc2_nat", [P, D, TAPS])
        wih_nat = sb("wih_nat", [P, 3, 2 * D])
        whh_nat = sb("whh_nat", [P, 3, D])
        wmsg_nat = sb("wmsg_nat", [P, D])
        wse_nat = sb("wse_nat", [SE, D])
        ident = sb("ident", [P, P])
        minus_half = sb("minus_half", [P, 1])
        minus_two = sb("minus_two", [P, 1])
        ones_k = sb("ones_k", [64, P], F32R)
        bias_k = sb("bias_k", [64, 2, MC], F32R)
        bias_hi = sb("bias_hi", [1, 2, MC], F32R)
        vec = sb("vec", [P, NVEC])
        var_eps = sb("var_eps", [P, 2])
        rstd_bn = sb("rstd_bn", [P, 2])
        scale_bn = sb("scale_bn", [P, 2])
        shift_bn = sb("shift_bn", [P, 2])
        mean_scaled = sb("mean_scaled", [P, 2])
        half_bias = sb("half_bias", [P, 2])
        sum_bias = sb("sum_bias", [P, 2])
        w_hi = sb("w_hi", [P, NW, P], F32R)
        w_lo = sb("w_lo", [P, NW, P], F32R)
        wm_hi = sb("wm_hi", [P, MC], F32R)
        wm_lo = sb("wm_lo", [P, MC], F32R)
        xT = sb("xT", [P, 2, N])
        xT_hi = sb("xT_hi", [P, 2, N], F32R)
        xT_lo = sb("xT_lo", [P, 2, N], F32R)
        h1 = sb("h1", [P, N])
        h1_hi = sb("h1_hi", [P, 2, N + 2 * PAD], F32R)
        h1_lo = sb("h1_lo", [P, 2, N + 2 * PAD], F32R)
        msg_hi = sb("msg_hi", [P, 2, NCH, D], F32R)
        msg_lo = sb("msg_lo", [P, 2, NCH, D], F32R)
        coord = sb("coord", [P, NCH, SE])
        coord_sq = sb("coord_sq", [P, NCH, SE])
        norm_part = sb("norm_part", [P, NCH, 1])
        norm_sq = sb("norm_sq", [P, NCH, 1])
        rows = sb("rows", [P, NCH, P])
        dist_lhs = sb("dist_lhs", [NK, N], F32R)
        dist_rhs = sb("dist_rhs", [NK, N], F32R)
        kern = sb("kern", [P, NCH, N])
        att = sb("att", [P, NCH, N])
        att_hi = sb("att_hi", [P, NCH, N], F32R)
        att_lo = sb("att_lo", [P, NCH, N], F32R)
        conv_sum = sb("conv_sum", [P, N])
        xc_hi = sb("xc_hi", [P, N], F32R)
        xc_lo = sb("xc_lo", [P, N], F32R)
        nmp_hi = sb("nmp_hi", [P, N], F32R)
        nmp_lo = sb("nmp_lo", [P, N], F32R)
        tanh_r = sb("tanh_r", [P, N])
        tanh_z = sb("tanh_z", [P, N])
        gh_n = sb("gh_n", [P, N])
        reset_gh = sb("reset_gh", [P, N])
        cand_in = sb("cand_in", [P, N])
        cand = sb("cand", [P, N])
        x_part = sb("x_part", [P, N])
        cand_part = sb("cand_part", [P, N])
        y2T = sb("y2T", [P, N])
        stats = sb("stats", [P, NCH, 6])
        mean_var = sb("mean_var", [P, NCH, 2])
        var4 = sb("var4", [P, NCH])
        eps4 = sb("eps4", [P, 1])
        rstd = sb("rstd", [P, NCH])
        o_nat = sb("o_nat", [P, NCH, D])

        ps_conv = bank("ps_conv")
        ps_dist = bank("ps_dist")
        ps_adj = bank("ps_adj")
        ps_acc = bank("ps_acc")
        ps_gate = bank("ps_gate", 4)
        R, Z, GI, GH = 0, 1, 2, 3
        ps_weights = [ps_conv, ps_dist, ps_adj, ps_acc]

        x_loaded = [sem(f"x_loaded{k}") for k in range(2)]
        adj_loaded = [sem(f"adj_loaded{k}") for k in range(2)]
        vec_loaded = sem("vec_loaded")
        bias_zeroed = sem("bias_zeroed")
        bias_loaded = sem("bias_loaded")
        wgate_loaded = sem("wgate_loaded")
        wmsg_loaded = sem("wmsg_loaded")
        wconv_loaded = sem("wconv_loaded")
        out_stored = sem("out_stored")
        ident_zero = sem("ident_zero")
        ident_made = sem("ident_made")
        consts_made = sem("consts_made")
        zeros_made = sem("zeros_made")
        vec_turned = sem("vec_turned")
        setup_dve = sem("setup_dve")
        bn_rstd = sem("bn_rstd")
        vec_ready = sem("vec_ready")
        wconv_scaled = sem("wconv_scaled")
        bias_k_ready = sem("bias_k_ready")
        w_turned = sem("w_turned")
        w_hi_made = sem("w_hi_made")
        w_lo_made = sem("w_lo_made")
        wm_turned = sem("wm_turned")
        wm_hi_made = sem("wm_hi_made")
        wm_lo_made = sem("wm_lo_made")
        x_turned = sem("x_turned")
        conv1_done = sem("conv1_done")
        msg_done = sem("msg_done")
        rows_turned = sem("rows_turned")
        dist_done = [sem(f"dist_done{c}") for c in range(NCH)]
        conv2_done = sem("conv2_done")
        nmp_done = sem("nmp_done")
        gh_done = sem("gh_done")
        r_done = sem("r_done")
        gi_done = sem("gi_done")
        z_done = sem("z_done")
        y_turned = sem("y_turned")
        xT_hi_made = sem("xT_hi_made")
        h1_hi_made = sem("h1_hi_made")
        msg_hi_made = sem("msg_hi_made")
        dist_lhs_made = sem("dist_lhs_made")
        kern_made = [sem(f"kern_made{c}") for c in range(NCH)]
        att_hi_made = [sem(f"att_hi_made{c}") for c in range(NCH)]
        xc_hi_made = sem("xc_hi_made")
        nmp_hi_made = sem("nmp_hi_made")
        gh_n_made = sem("gh_n_made")
        tanh_r_made = sem("tanh_r_made")
        tanh_z_made = sem("tanh_z_made")
        cand_made = sem("cand_made")
        xT_made = sem("xT_made")
        h1_made = sem("h1_made")
        msg_lo_made = sem("msg_lo_made")
        coord_made = sem("coord_made")
        coord_hi_made = sem("coord_hi_made")
        dist_rhs_made = sem("dist_rhs_made")
        att_made = [sem(f"att_made{c}") for c in range(NCH)]
        conv_sum_made = sem("conv_sum_made")
        xc_lo_made = sem("xc_lo_made")
        nmp_lo_made = sem("nmp_lo_made")
        reset_made = sem("reset_made")
        cand_in_made = sem("cand_in_made")
        x_part_made = sem("x_part_made")
        cand_part_made = sem("cand_part_made")
        y_made = sem("y_made")
        stats_made = sem("stats_made")
        mean_var_made = sem("mean_var_made")
        out_made = sem("out_made")
        xT_lo_made = sem("xT_lo_made")
        h1_lo_made = sem("h1_lo_made")
        pool_rows = sem("pool_rows")
        rows_made = sem("rows_made")
        att_lo_made = [sem(f"att_lo_made{c}") for c in range(NCH)]
        var4_made = sem("var4_made")
        rstd_made = sem("rstd_made")

        def done(j):
            return j + 1

        def landed(j, half):
            return 16 * half + 16

        def over_batches(eng, step, ahead=()):
            for b in (0, 1):
                step(b, 0, b, b == 0, False)
            with eng.Fori(1, B // 2 - 1) as half:
                for d in range(5):
                    eng.compute_val(half * 2 + d)
                for d in ahead:
                    eng.compute_val(half * 16 + d)
                for k in (0, 1):
                    step(half * 2 + k, half, k, False, False)
            for b in (B - 2, B - 1):
                step(b, b // 2, b % 2, False, b == B - 1)

        block = ctx.enter_context(nc.Block())

        @block.sync
        def _(sp):
            def load_x(j, k):
                sp.dma_start(x_nat[:, k], x[bass.ds(j, 1)].rearrange("o (c p) d -> p (o c) d", p=P)
                             ).then_inc(x_loaded[k], 16)

            def load_adj(j, k):
                sp.dma_start(adj_nat[:, k], adj[bass.ds(j, 1)].rearrange("o (c p) m -> p (o c) m", p=P)
                             ).then_inc(adj_loaded[k], 16)

            row = 0
            for name in VEC:
                n = w[name].shape[0] // P
                sp.dma_start(vec_rows[row:row + n, :], w[name].rearrange("(r p) -> r p", p=P)
                             ).then_inc(vec_loaded, 16)
                row += n
            load_x(0, 0)
            sp.dma_start(wmsg_nat[:, :], w["w_msg"]).then_inc(wmsg_loaded, 16)
            sp.dma_start(wse_nat[:, :], w["w_se"]).then_inc(wmsg_loaded, 16)
            sp.wait_ge(bias_zeroed, 1)
            for c in range(2):
                sp.dma_start(bias_row[:, c, 0:D], w["b_msg"].rearrange("(o d) -> o d", o=1)
                             ).then_inc(bias_loaded, 16)
                sp.dma_start(bias_row[:, c, D:D + SE], w["b_se"].rearrange("(o d) -> o d", o=1)
                             ).then_inc(bias_loaded, 16)
            sp.dma_start(wc1_nat[:, :], w["conv1_w"].rearrange("o i k -> o (i k)")).then_inc(wconv_loaded, 16)
            sp.dma_start(wc2_nat[:, :, :], w["conv2_w"]).then_inc(wconv_loaded, 16)
            sp.dma_start(wih_nat[:, :, :], w["w_ih"].rearrange("(g o) i -> o g i", o=P)
                         ).then_inc(wgate_loaded, 16)
            sp.dma_start(whh_nat[:, :, :], w["w_hh"].rearrange("(g o) i -> o g i", o=P)
                         ).then_inc(wgate_loaded, 16)
            load_adj(0, 0)
            load_x(1, 1)
            load_adj(1, 1)

            def store(j):
                sp.wait_ge(out_made, done(j))
                sp.dma_start(out[bass.ds(j, 1)].rearrange("o (c p) d -> p (o c) d", p=P), o_nat[:, :, :]
                             ).then_inc(out_stored, 16)

            def step(b, half, k, first, last):
                ahead = not (isinstance(b, int) and b >= B - 2)
                if ahead:
                    sp.wait_ge(x_turned, done(b))
                    load_x(b + 2, k)
                if not first:
                    store(b - 1)
                if ahead:
                    sp.wait_ge(dist_done[NCH - 1], done(b))
                    load_adj(b + 2, k)

            for b in (0, 1):
                step(b, 0, b, b == 0, False)
            with sp.Fori(1, B // 2 - 1) as half:
                for d in range(4):
                    sp.compute_val(half * 2 + d)
                for k in (0, 1):
                    for t, ahead in ((x, 2 + k), (out, k - 1), (adj, 2 + k)):
                        size = int(np.prod(t.shape[1:]))
                        sp.compute_val((half * 2 + ahead) * size)
                        sp.compute_val((half * 2 + ahead) * size * 4)
                for k in (0, 1):
                    step(half * 2 + k, half, k, False, False)
            for b in (B - 2, B - 1):
                step(b, b // 2, b % 2, False, b == B - 1)
            store(B - 1)
            sp.wait_ge(out_stored, 16 * B)

        @block.tensor
        def _(pe):
            def split_matmul(dst, lhs_hi, lhs_lo, rhs_hi, rhs_lo, start, stop):
                nc.tensor.matmul(dst, lhs_hi, rhs_hi, start=start, stop=False)
                nc.tensor.matmul(dst, lhs_hi, rhs_lo, start=False, stop=False)
                return nc.tensor.matmul(dst, lhs_lo, rhs_hi, start=False, stop=stop)

            def weight_matmul(dst, i, rhs_hi, rhs_lo, start, stop):
                return split_matmul(dst, w_hi[:, i, :], w_lo[:, i, :], rhs_hi, rhs_lo, start, stop)

            def turn_x(j, half, k, again):
                pe.wait_ge(x_loaded[k], landed(j, half))
                if again:
                    pe.wait_ge(tanh_r_made, done(j - 2))
                for c in range(NCH):
                    last = nc.tensor.transpose(ps_gate[:, R, c * P:(c + 1) * P], x_nat[:, k, c, :], ident[:, :])
                last.then_inc(x_turned, 1)

            def conv1(j, k, again):
                pe.wait_ge(xT_hi_made, done(j))
                pe.wait_ge(xT_lo_made, done(j))
                if again:
                    pe.wait_ge(tanh_z_made, done(j - 2))
                weight_matmul(ps_gate[:, Z, :], W_CONV1, xT_hi[:, k, :], xT_lo[:, k, :], True, True
                              ).then_inc(conv1_done, 1)

            def messages(j, k, again):
                if again:
                    pe.wait_ge(gh_n_made, done(j - 2))
                    pe.wait_ge(cand_in_made, done(j - 2))
                for g in (GI, GH):
                    dst = ps_gate[:, g, 0:2 * MC]
                    nc.tensor.matmul(dst, ones_k[:, :], bias_k[:, :, :].rearrange("k c m -> k (c m)"),
                                     start=True, stop=False)
                    for i in range(2):
                        c = 2 * (g - GI) + i
                        node = slice(c * P, (c + 1) * P)
                        last = split_matmul(ps_gate[:, g, i * MC:(i + 1) * MC], xT_hi[:, k, node],
                                            xT_lo[:, k, node], wm_hi[:, :], wm_lo[:, :], False, i == 1)
                last.then_inc(msg_done, 1)

            def turn_rows(j):
                pe.wait_ge(rows_made, done(j))
                pe.wait_ge(xT_made, done(j))
                for c in range(NCH):
                    last = nc.tensor.transpose(ps_gate[:, R, c * P:(c + 1) * P], rows[:, c, :], ident[:, :])
                last.then_inc(rows_turned, 1)

            def kernel_chunk(b, half, k, c, first):
                if c == 0:
                    pe.wait_ge(adj_loaded[k], landed(b, half))
                if c > 0:
                    pe.wait_ge(att_made[c - 1], done(b))
                elif not first:
                    pe.wait_ge(att_made[NCH - 1], done(b - 1))
                for n in range(NCH):
                    nc.tensor.transpose(ps_adj[:, n * P:(n + 1) * P], adj_nat[:, k, n, c * P:(c + 1) * P],
                                        ident[:, :])
                if c == 0:
                    pe.wait_ge(dist_lhs_made, done(b))
                    pe.wait_ge(dist_rhs_made, done(b))
                nc.tensor.matmul(ps_dist[:, :], dist_lhs[:, c * P:(c + 1) * P], dist_rhs[:, :],
                                 start=True, stop=True).then_inc(dist_done[c], 1)

            def conv2(b, k, taps, first):
                for t in taps:
                    if t == 0:
                        pe.wait_ge(h1_hi_made, done(b))
                        pe.wait_ge(h1_lo_made, done(b))
                        if not first:
                            pe.wait_ge(conv_sum_made, done(b - 1))
                    last = weight_matmul(ps_conv[:, :], W_CONV2 + t, h1_hi[:, k, t:t + N], h1_lo[:, k, t:t + N],
                                         t == 0, t == TAPS - 1)
                    if t == TAPS - 1:
                        last.then_inc(conv2_done, 1)

            def neighbours(b, k):
                for c in range(NCH):
                    pe.wait_ge(att_lo_made[c], done(b))
                    if c == 0:
                        pe.wait_ge(msg_lo_made, done(b))
                    last = split_matmul(ps_acc[:, :], msg_hi[:, k, c, :], msg_lo[:, k, c, :],
                                        att_hi[:, c, :], att_lo[:, c, :], c == 0, c == NCH - 1)
                last.then_inc(nmp_done, 1)

            def gates(b, k, last_batch):
                if not last_batch:
                    pe.wait_ge(h1_made, done(b + 1))
                    pe.wait_ge(dist_lhs_made, done(b + 1))
                    pe.wait_ge(dist_rhs_made, done(b + 1))
                    pe.wait_ge(msg_lo_made, done(b + 1))
                    pe.wait_ge(coord_made, done(b + 1))
                x2 = (xT_hi[:, k, :], xT_lo[:, k, :])
                weight_matmul(ps_gate[:, GH, :], W_HH + 2, *x2, True, True).then_inc(gh_done, 1)
                weight_matmul(ps_gate[:, R, :], W_HH, *x2, True, False)
                weight_matmul(ps_gate[:, Z, :], W_HH + 1, *x2, True, False)
                pe.wait_ge(xc_lo_made, done(b))
                xc = (xc_hi[:, :], xc_lo[:, :])
                weight_matmul(ps_gate[:, R, :], W_IH_X, *xc, False, False)
                weight_matmul(ps_gate[:, GI, :], W_IH_X + 2, *xc, True, False)
                weight_matmul(ps_gate[:, Z, :], W_IH_X + 1, *xc, False, False)
                pe.wait_ge(nmp_lo_made, done(b))
                nmp = (nmp_hi[:, :], nmp_lo[:, :])
                weight_matmul(ps_gate[:, R, :], W_IH_NMP, *nmp, False, True).then_inc(r_done, 1)
                weight_matmul(ps_gate[:, GI, :], W_IH_NMP + 2, *nmp, False, True).then_inc(gi_done, 1)
                weight_matmul(ps_gate[:, Z, :], W_IH_NMP + 1, *nmp, False, True).then_inc(z_done, 1)

            def turn_y(j):
                pe.wait_ge(y_made, done(j))
                for c in range(NCH):
                    last = nc.tensor.transpose(ps_acc[:, c * P:(c + 1) * P], y2T[:, c * P:(c + 1) * P], ident[:, :])
                last.then_inc(y_turned, 1)

            pe.wait_ge(ident_made, 1)
            pe.wait_ge(vec_loaded, 16 * len(VEC))
            nc.tensor.transpose(ps_gate[:, Z, 0:NVEC], vec_rows[:, :], ident[0:NVEC, 0:NVEC]
                                ).then_inc(vec_turned, 1)
            turn_x(0, 0, 0, False)
            pe.wait_ge(wmsg_loaded, 32)
            nc.tensor.transpose(ps_gate[:, GI, 0:D], wmsg_nat[:, :], ident[:, :])
            nc.tensor.transpose(ps_gate[:, GI, D:D + SE], wse_nat[:, :], ident[0:SE, 0:SE]
                                ).then_inc(wm_turned, 1)
            for i in range(NW):
                if i == 0:
                    pe.wait_ge(wgate_loaded, 32)
                if i == W_CONV1:
                    pe.wait_ge(wconv_scaled, 2)
                if i % 4 == 0 and i >= 16:
                    pe.wait_ge(w_lo_made, i // 4 - 3)
                if i < W_IH_NMP:
                    src = wih_nat[:, i - W_IH_X, 0:D]
                elif i < W_HH:
                    src = wih_nat[:, i - W_IH_NMP, D:2 * D]
                elif i < W_CONV1:
                    src = whh_nat[:, i - W_HH, :]
                elif i < W_CONV2:
                    src = wc1_nat[:, :]
                else:
                    src = wc2_nat[:, :, i - W_CONV2]
                turn = nc.tensor.transpose(ps_weights[i // 4 % 4][:, i % 4 * P:(i % 4 + 1) * P], src, ident[:, :])
                if i % 4 == 3 or i == NW - 1:
                    turn.then_inc(w_turned, 1)
            pe.wait_ge(wm_lo_made, 1)
            pe.wait_ge(bias_k_ready, 1)
            pe.wait_ge(xT_hi_made, 1)
            pe.wait_ge(xT_lo_made, 1)
            messages(0, 0, False)
            pe.wait_ge(w_lo_made, (NW + 3) // 4)
            conv1(0, 0, False)
            turn_rows(0)

            def step(b, half, k, first, last):
                nk, nhalf = 1 - k, half + k
                kernel_chunk(b, half, k, 0, first)
                conv2(b, k, range(0, 2), first)
                if not last:
                    turn_x(b + 1, nhalf, nk, not first)
                conv2(b, k, range(2, 4), first)
                kernel_chunk(b, half, k, 1, first)
                conv2(b, k, range(4, 7), first)
                if not last:
                    conv1(b + 1, nk, not first)
                    messages(b + 1, nk, not first)
                kernel_chunk(b, half, k, 2, first)
                conv2(b, k, range(7, 10), first)
                if not first:
                    turn_y(b - 1)
                kernel_chunk(b, half, k, 3, first)
                conv2(b, k, range(10, 14), first)
                if not last:
                    turn_rows(b + 1)
                conv2(b, k, range(14, TAPS), first)
                if not first:
                    pe.wait_ge(out_made, done(b - 1))
                neighbours(b, k)
                gates(b, k, last)

            over_batches(pe, step, (16, 32))
            turn_y(B - 1)

        @block.scalar
        def _(act):
            def hi_x(j, k, again):
                act.wait_ge(xT_made, done(j))
                if again:
                    act.wait_ge(gh_done, done(j - 2))
                    act.wait_ge(r_done, done(j - 2))
                nc.scalar.activation(xT_hi[:, k, :], xT[:, k, :], ACT.Copy).then_inc(xT_hi_made, 1)

            def hi_h1(j, k, again):
                act.wait_ge(h1_made, done(j))
                if again:
                    act.wait_ge(conv2_done, done(j - 2))
                nc.scalar.activation(h1_hi[:, k, PAD:PAD + N], h1[:, :], ACT.Copy).then_inc(h1_hi_made, 1)

            def hi_msg(j, k, again):
                act.wait_ge(msg_done, done(j))
                if again:
                    act.wait_ge(nmp_done, done(j - 2))
                src = ps_gate[:, GI:GH + 1, 0:2 * MC].rearrange("p g (i m) -> p g i m", i=2)[:, :, :, 0:D]
                nc.scalar.activation(msg_hi[:, k].rearrange("p (g i) d -> p g i d", i=2), src, ACT.Relu
                                     ).then_inc(msg_hi_made, 1)

            def lhs(j, again):
                act.wait_ge(rows_turned, done(j))
                if again:
                    act.wait_ge(dist_done[NCH - 1], done(j - 1))
                nc.scalar.activation(dist_lhs[:, :], ps_gate[0:NK, R, :], ACT.Copy).then_inc(dist_lhs_made, 1)

            def kernel_exp(b, c, first):
                act.wait_ge(dist_done[c], done(b))
                if not first:
                    act.wait_ge(att_made[c], done(b - 1))
                nc.scalar.activation(kern[:, c, :], ps_dist[:, :], ACT.Exp, scale=-1.0).then_inc(kern_made[c], 1)

            def hi_att(b, c, first):
                act.wait_ge(att_made[c], done(b))
                if not first:
                    act.wait_ge(nmp_done, done(b - 1))
                nc.scalar.activation(att_hi[:, c, :], att[:, c, :], ACT.Copy).then_inc(att_hi_made[c], 1)

            def branches(b, first):
                act.wait_ge(conv_sum_made, done(b))
                if not first:
                    act.wait_ge(z_done, done(b - 1))
                nc.scalar.activation(xc_hi[:, :], conv_sum[:, :], ACT.Relu).then_inc(xc_hi_made, 1)
                act.wait_ge(nmp_done, done(b))
                nc.scalar.activation(nmp_hi[:, :], ps_acc[:, :], ACT.Copy).then_inc(nmp_hi_made, 1)
                act.wait_ge(gh_done, done(b))
                if not first:
                    act.wait_ge(reset_made, done(b - 1))
                nc.scalar.activation(gh_n[:, :], ps_gate[:, GH, :], ACT.Identity, bias=vec[:, BHH + 2:BHH + 3]
                                     ).then_inc(gh_n_made, 1)

            def gate_tanh(j, again):
                act.wait_ge(r_done, done(j))
                nc.scalar.activation(tanh_r[:, :], ps_gate[:, R, :], ACT.Tanh, bias=half_bias[:, 0:1], scale=0.5
                                     ).then_inc(tanh_r_made, 1)
                act.wait_ge(z_done, done(j))
                if again:
                    act.wait_ge(cand_part_made, done(j - 1))
                nc.scalar.activation(tanh_z[:, :], ps_gate[:, Z, :], ACT.Tanh, bias=half_bias[:, 1:2], scale=0.5
                                     ).then_inc(tanh_z_made, 1)

            def candidate(j, again):
                act.wait_ge(cand_in_made, done(j))
                if again:
                    act.wait_ge(cand_part_made, done(j - 1))
                nc.scalar.activation(cand[:, :], cand_in[:, :], ACT.Tanh, bias=vec[:, BIH + 2:BIH + 3]
                                     ).then_inc(cand_made, 1)

            hi_x(0, 0, False)
            act.wait_ge(wm_turned, 1)
            act.wait_ge(zeros_made, 1)
            nc.scalar.activation(wm_hi[:, 0:D + SE], ps_gate[:, GI, 0:D + SE], ACT.Copy).then_inc(wm_hi_made, 1)
            for i in range(0, NW, 4):
                n = min(4, NW - i)
                act.wait_ge(w_turned, i // 4 + 1)
                nc.scalar.activation(w_hi[:, i:i + n, :].rearrange("p a b -> p (a b)"),
                                     ps_weights[i // 4 % 4][:, 0:n * P], ACT.Copy).then_inc(w_hi_made, 1)
            act.wait_ge(vec_ready, 1)
            hi_msg(0, 0, False)
            hi_h1(0, 0, False)
            lhs(0, False)

            def step(b, half, k, first, last):
                nk = 1 - k
                if not first:
                    gate_tanh(b - 1, not (isinstance(b, int) and b == 1))
                kernel_exp(b, 0, first)
                if not first:
                    candidate(b - 1, not (isinstance(b, int) and b == 1))
                if not last:
                    hi_x(b + 1, nk, not first)
                hi_att(b, 0, first)
                kernel_exp(b, 1, first)
                hi_att(b, 1, first)
                if not last:
                    hi_h1(b + 1, nk, not first)
                    hi_msg(b + 1, nk, not first)
                for c in (2, 3):
                    kernel_exp(b, c, first)
                    hi_att(b, c, first)
                if not last:
                    lhs(b + 1, True)
                branches(b, first)

            over_batches(act, step)
            gate_tanh(B - 1, True)
            candidate(B - 1, True)

        @block.vector
        def _(dve):
            def take_x(j, k, again):
                dve.wait_ge(x_turned, done(j))
                if again:
                    dve.wait_ge(x_part_made, done(j - 2))
                nc.vector.tensor_copy(xT[:, k, :], ps_gate[:, R, :]).then_inc(xT_made, 1)

            def take_h1(j, again):
                dve.wait_ge(conv1_done, done(j))
                if again:
                    dve.wait_ge(h1_lo_made, done(j - 1))
                nc.vector.tensor_scalar(h1[:, :], ps_gate[:, Z, :], shift_bn[:, 0:1], 0.0, ALU.add, ALU.max
                                        ).then_inc(h1_made, 1)

            def take_msg(j, k, again):
                dve.wait_ge(msg_hi_made, done(j))
                if again:
                    dve.wait_ge(rows_made, done(j - 1))
                src = ps_gate[:, GI:GH + 1, 0:2 * MC].rearrange("p g (i m) -> p g i m", i=2)[:, :, :, D:D + SE]
                nc.vector.tensor_copy(coord[:, :, :].rearrange("p (g i) s -> p g i s", i=2), src
                                      ).then_inc(coord_made, 1)
                for g in range(2):
                    src = ps_gate[:, GI + g, 0:2 * MC].rearrange("p (i m) -> p i m", i=2)[:, :, 0:D]
                    last = nc.vector.scalar_tensor_tensor(
                        out=msg_lo[:, k, 2 * g:2 * g + 2, :], in0=src, scalar=0.0,
                        in1=msg_hi[:, k, 2 * g:2 * g + 2, :].bitcast(F32), op0=ALU.max, op1=ALU.subtract)
                last.then_inc(msg_lo_made, 1)
                dve.wait_ge(coord_made, done(j))
                if again:
                    dve.wait_ge(rows_turned, done(j - 1))
                nc.vector.tensor_copy(
                    rows[:, :, 0:2 * SE].bitcast(F32R).rearrange("p c (r s) -> p c r s", s=SE),
                    coord[:, :, :].rearrange("p c (r s) -> p c r s", r=1).to_broadcast([P, NCH, 2, SE])
                ).then_inc(coord_hi_made, 1)

            def rhs(j, again):
                dve.wait_ge(rows_turned, done(j))
                if again:
                    dve.wait_ge(dist_done[NCH - 1], done(j - 1))
                nc.vector.tensor_copy(dist_rhs[:, :], ps_gate[RHS:RHS + NK, R, :]).then_inc(dist_rhs_made, 1)

            def mask(b, c, first):
                dve.wait_ge(kern_made[c], done(b))
                if not first:
                    dve.wait_ge(att_lo_made[c], done(b - 1))
                nc.vector.tensor_tensor(att[:, c, :], kern[:, c, :], ps_adj[:, :], ALU.mult
                                        ).then_inc(att_made[c], 1)

            def branches(b, k, first):
                dve.wait_ge(conv2_done, done(b))
                nc.vector.scalar_tensor_tensor(out=conv_sum[:, :], in0=ps_conv[:, :], scalar=shift_bn[:, 1:2],
                                               in1=xT[:, k, :], op0=ALU.add, op1=ALU.add
                                               ).then_inc(conv_sum_made, 1)
                dve.wait_ge(xc_hi_made, done(b))
                nc.vector.scalar_tensor_tensor(out=xc_lo[:, :], in0=conv_sum[:, :], scalar=0.0,
                                               in1=xc_hi[:, :].bitcast(F32), op0=ALU.max, op1=ALU.subtract
                                               ).then_inc(xc_lo_made, 1)
                dve.wait_ge(nmp_hi_made, done(b))
                nc.vector.tensor_tensor(nmp_lo[:, :], ps_acc[:, :], nmp_hi[:, :].bitcast(F32), ALU.subtract
                                        ).then_inc(nmp_lo_made, 1)

            def reset(j):
                dve.wait_ge(gh_n_made, done(j))
                dve.wait_ge(tanh_r_made, done(j))
                nc.vector.scalar_tensor_tensor(out=reset_gh[:, :], in0=tanh_r[:, :], scalar=1.0, in1=gh_n[:, :],
                                               op0=ALU.add, op1=ALU.mult).then_inc(reset_made, 1)
                dve.wait_ge(gi_done, done(j))
                dve.wait_ge(reset_made, done(j))
                nc.vector.scalar_tensor_tensor(out=cand_in[:, :], in0=reset_gh[:, :], scalar=0.5,
                                               in1=ps_gate[:, GI, :], op0=ALU.mult, op1=ALU.add
                                               ).then_inc(cand_in_made, 1)

            def blend_x(j, k):
                dve.wait_ge(tanh_z_made, done(j))
                nc.vector.scalar_tensor_tensor(out=x_part[:, :], in0=tanh_z[:, :], scalar=3.0, in1=xT[:, k, :],
                                               op0=ALU.add, op1=ALU.mult).then_inc(x_part_made, 1)

            def blend_cand(j):
                dve.wait_ge(cand_made, done(j))
                nc.vector.scalar_tensor_tensor(out=cand_part[:, :], in0=tanh_z[:, :], scalar=1.0, in1=cand[:, :],
                                               op0=ALU.subtract, op1=ALU.mult).then_inc(cand_part_made, 1)
                dve.wait_ge(cand_part_made, done(j))
                nc.vector.tensor_tensor(y2T[:, :], x_part[:, :], cand_part[:, :], ALU.subtract
                                        ).then_inc(y_made, 1)

            def statistics(j):
                dve.wait_ge(y_turned, done(j))
                for c in range(NCH):
                    last = nc.vector.bn_stats(stats[:, c, :], ps_acc[:, c * P:(c + 1) * P])
                last.then_inc(stats_made, 1)

            def aggregate(j):
                for c in range(NCH):
                    last = nc.vector.bn_aggr(mean_var[:, c, :], stats[:, c, :])
                last.then_inc(mean_var_made, 1)

            def normalise(j, again):
                dve.wait_ge(rstd_made, done(j))
                if again:
                    dve.wait_ge(out_stored, 16 * j)
                for c in range(NCH):
                    last = nc.vector.tensor_scalar(o_nat[:, c, :], ps_acc[:, c * P:(c + 1) * P],
                                                   mean_var[:, c, 0:1], rstd[:, c:c + 1],
                                                   ALU.subtract, ALU.mult)
                last.then_inc(out_made, 1)

            dve.wait_ge(vec_turned, 1)
            nc.vector.tensor_copy(vec[:, :], ps_gate[:, Z, 0:NVEC]).then_inc(setup_dve, 1)
            dve.wait_ge(setup_dve, 1)
            nc.vector.tensor_scalar(var_eps[:, :], vec[:, V1:V2 + 1:V2 - V1], EPS, None, ALU.add
                                    ).then_inc(setup_dve, 1)
            nc.vector.tensor_tensor(sum_bias[:, :], vec[:, BIH:BIH + 2], vec[:, BHH:BHH + 2], ALU.add
                                    ).then_inc(setup_dve, 1)
            dve.wait_ge(setup_dve, 3)
            nc.vector.tensor_scalar(half_bias[:, :], sum_bias[:, :], 0.5, None, ALU.mult).then_inc(setup_dve, 1)
            take_x(0, 0, False)
            dve.wait_ge(bn_rstd, 1)
            nc.vector.tensor_tensor(scale_bn[:, :], vec[:, G1:G2 + 1:G2 - G1], rstd_bn[:, :], ALU.mult
                                    ).then_inc(setup_dve, 1)
            dve.wait_ge(setup_dve, 5)
            nc.vector.tensor_tensor(mean_scaled[:, :], vec[:, M1:M2 + 1:M2 - M1], scale_bn[:, :], ALU.mult
                                    ).then_inc(setup_dve, 1)
            dve.wait_ge(wconv_loaded, 32)
            nc.vector.tensor_scalar(wc1_nat[:, :], wc1_nat[:, :], scale_bn[:, 0:1], None, ALU.mult
                                    ).then_inc(wconv_scaled, 1)
            nc.vector.tensor_scalar(wc2_nat[:, :, :], wc2_nat[:, :, :], scale_bn[:, 1:2], None, ALU.mult
                                    ).then_inc(wconv_scaled, 1)
            dve.wait_ge(setup_dve, 6)
            nc.vector.tensor_tensor(shift_bn[:, :], vec[:, B1:B2 + 1:B2 - B1], mean_scaled[:, :], ALU.subtract
                                    ).then_inc(vec_ready, 1)
            dve.wait_ge(wm_hi_made, 1)
            dve.wait_ge(zeros_made, 1)
            nc.vector.tensor_tensor(wm_lo[:, 0:D + SE], ps_gate[:, GI, 0:D + SE],
                                    wm_hi[:, 0:D + SE].bitcast(F32), ALU.subtract).then_inc(wm_lo_made, 1)
            dve.wait_ge(bias_loaded, 64)
            nc.vector.tensor_copy(bias_hi[:, :, :], bias_row[:, :, :]).then_inc(setup_dve, 1)
            dve.wait_ge(setup_dve, 7)
            nc.vector.tensor_copy(bias_k[0:1, :, :], bias_hi[:, :, :].bitcast(F32)).then_inc(setup_dve, 1)
            nc.vector.tensor_tensor(bias_k[32:33, :, :], bias_row[:, :, :], bias_hi[:, :, :].bitcast(F32),
                                    ALU.subtract).then_inc(bias_k_ready, 1)
            for i in range(0, NW, 4):
                n = min(4, NW - i)
                dve.wait_ge(w_hi_made, i // 4 + 1)
                nc.vector.tensor_tensor(w_lo[:, i:i + n, :].rearrange("p a b -> p (a b)"),
                                        ps_weights[i // 4 % 4][:, 0:n * P],
                                        w_hi[:, i:i + n, :].bitcast(F32).rearrange("p a b -> p (a b)"),
                                        ALU.subtract).then_inc(w_lo_made, 1)
            dve.wait_ge(vec_ready, 1)
            take_msg(0, 0, False)
            take_h1(0, False)
            rhs(0, False)

            def step(b, half, k, first, last):
                nk = 1 - k
                if not first:
                    reset(b - 1)
                    blend_x(b - 1, nk)
                mask(b, 0, first)
                if not last:
                    take_x(b + 1, nk, not first)
                mask(b, 1, first)
                if not first:
                    blend_cand(b - 1)
                if not last:
                    take_h1(b + 1, True)
                    take_msg(b + 1, nk, True)
                mask(b, 2, first)
                if not first:
                    statistics(b - 1)
                    dve.wait_ge(stats_made, done(b - 1))
                mask(b, 3, first)
                if not first:
                    aggregate(b - 1)
                    normalise(b - 1, not (isinstance(b, int) and b == 1))
                if not last:
                    rhs(b + 1, True)
                branches(b, k, first)

            over_batches(dve, step, (0, 16))
            reset(B - 1)
            blend_x(B - 1, (B - 1) % 2)
            blend_cand(B - 1)
            statistics(B - 1)
            dve.wait_ge(stats_made, B)
            aggregate(B - 1)
            normalise(B - 1, True)

        @block.gpsimd
        def _(pool):
            def lo_x(j, k):
                pool.wait_ge(xT_hi_made, done(j))
                nc.gpsimd.tensor_tensor(xT_lo[:, k, :], xT[:, k, :], xT_hi[:, k, :].bitcast(F32), ALU.subtract
                                        ).then_inc(xT_lo_made, 1)

            def lo_h1(j, k):
                pool.wait_ge(h1_hi_made, done(j))
                nc.gpsimd.tensor_tensor(h1_lo[:, k, PAD:PAD + N], h1[:, :], h1_hi[:, k, PAD:PAD + N].bitcast(F32),
                                        ALU.subtract).then_inc(h1_lo_made, 1)

            def lo_att(b, c):
                pool.wait_ge(att_hi_made[c], done(b))
                nc.gpsimd.tensor_tensor(att_lo[:, c, :], att[:, c, :], att_hi[:, c, :].bitcast(F32), ALU.subtract
                                        ).then_inc(att_lo_made[c], 1)

            def make_rows(j):
                hi = rows[:, :, 0:SE]
                lo = rows[:, :, 2 * SE:3 * SE]
                moving = rows[:, :, RHS:RHS + 4 * SE].rearrange("p c (r h s) -> p c r h s", h=2, s=SE)

                def twice(v):
                    return v.rearrange("p c (r s) -> p c r s", r=1).to_broadcast([P, NCH, 2, SE])

                tt = nc.gpsimd.tensor_tensor
                pool.wait_ge(coord_hi_made, done(j))
                tt(rows[:, :, 2 * SE:4 * SE].rearrange("p c (r s) -> p c r s", s=SE), twice(coord[:, :, :]),
                   twice(hi), ALU.subtract)
                tt(coord_sq[:, :, :], coord[:, :, :], coord[:, :, :], ALU.mult)
                m2 = minus_two[:, :].rearrange("p (c r s) -> p c r s", c=1, r=1)
                tt(moving[:, :, :, 0, :], twice(hi), m2.to_broadcast([P, NCH, 2, SE]), ALU.mult
                   ).then_inc(pool_rows, 1)
                pool.wait_ge(pool_rows, 3 * j + 1)
                tt(moving[:, :, :, 1, :], twice(lo), m2.to_broadcast([P, NCH, 2, SE]), ALU.mult)
                tt(norm_part[:, :, :], coord_sq[:, :, 0:1], coord_sq[:, :, 1:2], ALU.add
                   ).then_inc(pool_rows, 1)
                pool.wait_ge(pool_rows, 3 * j + 2)
                both = rows[:, :, SQ:RHS + ONE + 1:RHS + ONE - SQ]
                both_lo = rows[:, :, SQ + 1:RHS + ONE + 2:RHS + ONE - SQ]
                tt(both.bitcast(F32R), norm_part[:, :, :].to_broadcast([P, NCH, 2]),
                   coord_sq[:, :, 2:3].to_broadcast([P, NCH, 2]), ALU.add)
                tt(norm_sq[:, :, :], norm_part[:, :, :], coord_sq[:, :, 2:3], ALU.add).then_inc(pool_rows, 1)
                pool.wait_ge(pool_rows, 3 * j + 3)
                tt(both_lo, norm_sq[:, :, :].to_broadcast([P, NCH, 2]), both, ALU.subtract
                   ).then_inc(rows_made, 1)

            def inverse_std(j, again):
                pool.wait_ge(mean_var_made, done(j))
                if again:
                    pool.wait_ge(out_made, done(j - 1))
                nc.gpsimd.tensor_tensor(var4[:, :], mean_var[:, :, 1], eps4[:, :].to_broadcast([P, NCH]), ALU.add
                                        ).then_inc(var4_made, 1)
                pool.wait_ge(var4_made, done(j))
                nc.gpsimd.tensor_tensor(rstd[:, :], var4[:, :], minus_half[:, :].to_broadcast([P, NCH]), ALU.pow
                                        ).then_inc(rstd_made, 1)

            pool.memset(bias_row[:, :, :], 0.0).then_inc(bias_zeroed, 1)
            pool.memset(ident[:, :], 0.0).then_inc(ident_zero, 1)
            pool.wait_ge(ident_zero, 1)
            pool.affine_select(out=ident[:, :], in_=ident[:, :], compare_op=ALU.not_equal, fill=1.0, base=0,
                               pattern=[[-1, P]], channel_multiplier=1).then_inc(ident_made, 1)
            pool.memset(minus_half[:, :], -0.5)
            pool.memset(minus_two[:, :], -2.0)
            pool.memset(eps4[:, :], 4 * EPS).then_inc(consts_made, 1)
            pool.memset(wm_hi[:, :].bitcast(F32), 0.0)
            pool.memset(wm_lo[:, :].bitcast(F32), 0.0)
            pool.memset(bias_k[:, :, :].bitcast(F32), 0.0)
            pool.memset(ones_k[:, :].bitcast(F32), 1.0)
            pool.memset(rows[:, :, :], 0.0).then_inc(ident_zero, 1)
            for t in (h1_hi, h1_lo):
                pool.memset(t[:, :, 0:PAD].bitcast(F32), 0.0)
                pool.memset(t[:, :, PAD + N:].bitcast(F32), 0.0)
            pool.wait_ge(ident_zero, 2)
            pool.memset(rows[:, :, ONE:ONE + 2], 1.0)
            pool.memset(rows[:, :, RHS + SQ:RHS + SQ + 2], 1.0).then_inc(zeros_made, 1)
            pool.wait_ge(consts_made, 1)
            pool.wait_ge(setup_dve, 2)
            nc.gpsimd.tensor_tensor(rstd_bn[:, :], var_eps[:, :], minus_half[:, :].to_broadcast([P, 2]), ALU.pow
                                    ).then_inc(bn_rstd, 1)
            lo_x(0, 0)
            make_rows(0)
            lo_h1(0, 0)

            def step(b, half, k, first, last):
                nk = 1 - k
                if not last:
                    lo_x(b + 1, nk)
                lo_att(b, 0)
                lo_att(b, 1)
                if not last:
                    lo_h1(b + 1, nk)
                    make_rows(b + 1)
                lo_att(b, 2)
                if not first:
                    inverse_std(b - 1, not (isinstance(b, int) and b == 1))
                lo_att(b, 3)

            for b in (0, 1):
                step(b, 0, b, b == 0, False)
            with pool.Fori(1, B // 2 - 1) as half:
                for d in range(4):
                    pool.compute_val(half * 2 + d)
                for d in range(4, 10):
                    pool.compute_val(half * 6 + d)
                for k in (0, 1):
                    step(half * 2 + k, half, k, False, False)
            for b in (B - 2, B - 1):
                step(b, b // 2, b % 2, False, b == B - 1)
            inverse_std(B - 1, True)


def kernel(**inputs):
    import numpy as _np
    import concourse.bacc as _bacc
    from concourse import mybir as _mybir
    from concourse.bass_utils import run_bass_kernel_spmd as _run

    nc = _bacc.Bacc("TRN2", target_bir_lowering=False, num_devices=1)
    arrays, aps = {}, {}
    for name, value in inputs.items():
        a = _np.ascontiguousarray(value)
        arrays[f"in_{name}_dram"] = a
        aps[name] = nc.dram_tensor(f"in_{name}_dram", a.shape, _mybir.dt.from_np(a.dtype), kind="ExternalInput").ap()
    shape = tuple(arrays["in_x_dram"].shape)
    out = nc.dram_tensor("out_0_dram", shape, _mybir.dt.from_np(_np.dtype("float32")), kind="ExternalOutput").ap()
    gnn_program(nc, aps, out)
    r = _run(nc, [arrays], core_ids=[0])
    return r.results[0]["out_0_dram"]
```

```python
from contextlib import ExitStack

import numpy as np
import concourse.bass as bass
from concourse import mybir

F32 = mybir.dt.float32
F32R = mybir.dt.float32r
ALU = mybir.AluOpType
ACT = mybir.ActivationFunctionType

EPS = 1e-5
P = 128
WARM_UP = 8


TAPS = 17
VEC = ["bn1_g", "bn1_b", "bn1_m", "bn1_v", "bn2_g", "bn2_b", "bn2_m", "bn2_v", "b_ih", "b_hh"]
G1, B1, M1, V1, G2, B2, M2, V2, BIH, BHH, NVEC = 0, 1, 2, 3, 4, 5, 6, 7, 8, 11, 14


def gnn_program(nc, xT_in, maskT_in, vec_in, conv_in, gate_in, msg_in, msg_bias_in, out):
    B, D, N = xT_in.shape
    NCH = N // P
    MC = msg_in.shape[1]
    SE = MC - 1 - D
    assert D == P and N == 512 and B % 2 == 0 and B >= 6 and SE == 3
    HALF = N // 2
    EVEN, ODD = (TAPS + 1) // 2, TAPS // 2
    PAD = TAPS // 4
    PHASE = PAD + HALF + PAD + 2
    RW = HALF + 2

    NK = 4 * SE + 4
    SQ, ONE = 4 * SE, 4 * SE + 2
    RHS = 32

    W_CONV1 = 0
    W_ODD = 1
    W_EVEN = W_ODD + ODD
    W_SUM = W_EVEN + EVEN - 1
    W_IH_X = W_SUM + EVEN
    W_IH_NMP, W_HH = W_IH_X + 3, W_IH_X + 6
    NW = W_IH_X + 9
    GROUPS = [(W_CONV1, 1), (W_ODD, 4), (W_ODD + 4, 4), (W_EVEN, 5), (W_EVEN + 5, 4),
              (W_SUM + 1, 4), (W_SUM + 5, 4), (W_HH, 3), (W_IH_X, 3), (W_IH_NMP, 3)]
    W_IN_CONV = W_SUM + 1

    with ExitStack() as ctx:
        def sb(name, shape, dt=F32):
            return ctx.enter_context(nc.sbuf_tensor(name, shape, dt))

        def bank(name, n=1):
            return ctx.enter_context(nc.psum_tensor(name, [P, 512] if n == 1 else [P, n, 512], F32))

        def sem(name):
            return ctx.enter_context(nc.semaphore(name))

        xT_new = sb("xT_new", [P, 2, N])
        maskT = sb("maskT", [P, 2, NCH, N])
        vec = sb("vec", [P, NVEC])
        msg_bias = sb("msg_bias", [P, MC])
        w_all = sb("w_all", [P, NW, P])
        wm = sb("wm", [P, MC])
        warm_zero = sb("warm_zero", [P, N], F32R)
        ident = sb("ident", [P, P])
        minus_half = sb("minus_half", [P, 1])
        minus_two = sb("minus_two", [P, 1])
        var_eps = sb("var_eps", [P, 2])
        rstd_bn = sb("rstd_bn", [P, 2])
        scale_bn = sb("scale_bn", [P, 2])
        shift_bn = sb("shift_bn", [P, 2])
        mean_scaled = sb("mean_scaled", [P, 2])
        half_bias = sb("half_bias", [P, 2])
        sum_bias = sb("sum_bias", [P, 2])
        w_hi = sb("w_hi", [P, NW, P], F32R)
        w_lo = sb("w_lo", [P, NW, P], F32R)
        wm_split = sb("wm_split", [P, 2, MC], F32R)
        xT = sb("xT", [P, 2, N])
        x_shift = sb("x_shift", [P, 2, N])
        xT_hi = sb("xT_hi", [P, 2, N], F32R)
        xT_lo = sb("xT_lo", [P, 2, N], F32R)
        h1 = sb("h1", [P, 3, HALF])
        h1_hi = sb("h1_hi", [P, 2, 3, PHASE], F32R)
        h1_lo = sb("h1_lo", [P, 2, 3, PHASE], F32R)
        msg_hi = sb("msg_hi", [P, 2, NCH, D], F32R)
        msg_lo = sb("msg_lo", [P, 2, NCH, D], F32R)
        msg_part = sb("msg_part", [P, NCH, MC])
        msg_sum = sb("msg_sum", [P, NCH, MC])
        coord_sq = sb("coord_sq", [P, NCH, SE])
        norm_part = sb("norm_part", [P, NCH, 1])
        norm_sq = sb("norm_sq", [P, NCH, 1])
        rows = sb("rows", [P, NCH, P])
        dist_lhs = sb("dist_lhs", [NK, N], F32R)
        dist_rhs = sb("dist_rhs", [NK, N], F32R)
        kern = sb("kern", [P, NCH, N])
        att = sb("att", [P, NCH, N])
        att_hi = sb("att_hi", [P, NCH, N], F32R)
        att_lo = sb("att_lo", [P, NCH, N], F32R)
        even_part = sb("even_part", [P, HALF])
        odd_part = sb("odd_part", [P, HALF])
        odd_neg = sb("odd_neg", [P, HALF])
        conv_sum = sb("conv_sum", [P, N])
        xc_hi = sb("xc_hi", [P, N], F32R)
        xc_lo = sb("xc_lo", [P, N], F32R)
        nmp_hi = sb("nmp_hi", [P, N], F32R)
        nmp_lo = sb("nmp_lo", [P, N], F32R)
        tanh_r = sb("tanh_r", [P, N])
        tanh_z = sb("tanh_z", [P, N])
        gh_n = sb("gh_n", [P, N])
        reset_gh = sb("reset_gh", [P, N])
        cand_in = sb("cand_in", [P, N])
        cand = sb("cand", [P, N])
        x_part = sb("x_part", [P, N])
        cand_part = sb("cand_part", [P, N])
        y2T = sb("y2T", [P, N])
        stats = sb("stats", [P, NCH, 6])
        mean_var = sb("mean_var", [P, NCH, 2])
        var4 = sb("var4", [P, NCH])
        eps4 = sb("eps4", [P, 1])
        rstd = sb("rstd", [P, NCH])
        o_nat = sb("o_nat", [P, NCH, D])

        ps_conv = bank("ps_conv")
        ps_dist = bank("ps_dist", 2)
        ps_acc = bank("ps_acc")
        ps_gate = bank("ps_gate", 4)
        R, Z, GI, GH = 0, 1, 2, 3

        x_loaded = [sem(f"x_loaded{k}") for k in range(2)]
        mask_loaded = [sem(f"mask_loaded{k}") for k in range(2)]
        vec_loaded = sem("vec_loaded")
        bias_loaded = sem("bias_loaded")
        wmsg_loaded = sem("wmsg_loaded")
        wconv1_loaded = sem("wconv1_loaded")
        wodd_loaded = sem("wodd_loaded")
        weven_loaded = sem("weven_loaded")
        wgate_loaded = sem("wgate_loaded")
        out_stored = sem("out_stored")
        warm_zeroed = sem("warm_zeroed")
        ident_zero = sem("ident_zero")
        ident_made = sem("ident_made")
        consts_made = sem("consts_made")
        rows_zeroed = sem("rows_zeroed")
        zeros_made = sem("zeros_made")
        setup_dve = sem("setup_dve")
        bn_rstd = sem("bn_rstd")
        vec_ready = sem("vec_ready")
        wsum_made = sem("wsum_made")
        w_hi_made = [sem(f"w_hi_made{g}") for g in range(len(GROUPS))]
        w_lo_made = [sem(f"w_lo_made{g}") for g in range(len(GROUPS))]
        wm_hi_made = sem("wm_hi_made")
        wm_lo_made = sem("wm_lo_made")
        conv1_done = sem("conv1_done")
        msg_done = sem("msg_done")
        rows_turned = sem("rows_turned")
        dist_done = [sem(f"dist_done{c}") for c in range(NCH)]
        conv_r_done = sem("conv_r_done")
        conv2_done = sem("conv2_done")
        nmp_done = sem("nmp_done")
        gh_done = sem("gh_done")
        r_done = sem("r_done")
        gi_done = sem("gi_done")
        z_done = sem("z_done")
        y_turned = sem("y_turned")
        xT_hi_made = sem("xT_hi_made")
        x_shift_made = sem("x_shift_made")
        h1_taken = sem("h1_taken")
        msg_hi_made = sem("msg_hi_made")
        dist_lhs_made = sem("dist_lhs_made")
        kern_made = [sem(f"kern_made{c}") for c in range(NCH)]
        att_hi_made = [sem(f"att_hi_made{c}") for c in range(NCH)]
        xc_hi_made = sem("xc_hi_made")
        nmp_hi_made = sem("nmp_hi_made")
        gh_n_made = sem("gh_n_made")
        tanh_r_made = sem("tanh_r_made")
        tanh_z_made = sem("tanh_z_made")
        cand_made = sem("cand_made")
        xT_made = sem("xT_made")
        h1_made = sem("h1_made")
        h1_hi_made = sem("h1_hi_made")
        h1_odd_split = sem("h1_odd_split")
        h1_hi_even = sem("h1_hi_even")
        msg_lo_made = sem("msg_lo_made")
        msg_part_made = sem("msg_part_made")
        msg_sum_made = sem("msg_sum_made")
        coord_hi_made = sem("coord_hi_made")
        dist_rhs_made = sem("dist_rhs_made")
        att_made = [sem(f"att_made{c}") for c in range(NCH)]
        odd_part_made = sem("odd_part_made")
        odd_neg_made = sem("odd_neg_made")
        conv_sum_made = sem("conv_sum_made")
        xc_lo_made = sem("xc_lo_made")
        nmp_lo_made = sem("nmp_lo_made")
        reset_made = sem("reset_made")
        cand_in_made = sem("cand_in_made")
        x_part_made = sem("x_part_made")
        cand_part_made = sem("cand_part_made")
        y_made = sem("y_made")
        stats_made = sem("stats_made")
        mean_var_made = sem("mean_var_made")
        out_made = sem("out_made")
        xT_lo_made = sem("xT_lo_made")
        h1_lo_made = sem("h1_lo_made")
        pool_rows = sem("pool_rows")
        rows_made = sem("rows_made")
        att_lo_made = [sem(f"att_lo_made{c}") for c in range(NCH)]
        var4_made = sem("var4_made")
        rstd_made = sem("rstd_made")

        def done(j):
            return j + 1

        def landed(half):
            return 16 * half + 16

        def over_batches(eng, step, ahead=()):
            for b in (0, 1):
                step(b, 0, b, b == 0, False)
            with eng.Fori(1, B // 2 - 1) as half:
                for d in range(5):
                    eng.compute_val(half * 2 + d)
                for d in ahead:
                    eng.compute_val(half * 16 + d)
                for k in (0, 1):
                    step(half * 2 + k, half, k, False, False)
            for b in (B - 2, B - 1):
                step(b, b // 2, b % 2, False, b == B - 1)

        block = ctx.enter_context(nc.Block())

        @block.sync
        def _(sp):
            def load_x(j, k):
                sp.dma_start(xT_new[:, k], xT_in[bass.ds(j, 1)].rearrange("o p n -> p (o n)")
                             ).then_inc(x_loaded[k], 16)

            def load_mask(j, k):
                sp.dma_start(maskT[:, k], maskT_in[bass.ds(j, 1)].rearrange("o p c n -> p (o c) n")
                             ).then_inc(mask_loaded[k], 16)

            load_x(0, 0)
            sp.dma_start(w_all[:, W_CONV1, :], conv_in[:, W_CONV1, :]).then_inc(wconv1_loaded, 16)
            sp.dma_start(vec[:, :], vec_in).then_inc(vec_loaded, 16)
            sp.dma_start(wm[:, :], msg_in).then_inc(wmsg_loaded, 16)
            sp.dma_start(w_all[:, W_ODD:W_EVEN, :], conv_in[:, W_ODD:W_EVEN, :]).then_inc(wodd_loaded, 16)
            sp.dma_start(msg_bias[:, :], msg_bias_in).then_inc(bias_loaded, 16)
            sp.dma_start(w_all[:, W_EVEN:W_IN_CONV, :], conv_in[:, W_EVEN:W_IN_CONV, :]
                         ).then_inc(weven_loaded, 16)
            load_x(1, 1)
            load_mask(0, 0)
            sp.dma_start(w_all[:, W_IH_X:NW, :], gate_in).then_inc(wgate_loaded, 16)
            load_mask(1, 1)

            def store(j):
                sp.wait_ge(out_made, done(j))
                sp.dma_start(out[bass.ds(j, 1)].rearrange("o p c d -> p (o c) d"), o_nat[:, :, :]
                             ).then_inc(out_stored, 16)

            def step(b, half, k, first, last):
                ahead = not (isinstance(b, int) and b >= B - 2)
                if ahead:
                    sp.wait_ge(xT_lo_made, done(b))
                    sp.wait_ge(x_shift_made, done(b))
                    sp.wait_ge(xT_made, done(b))
                    load_x(b + 2, k)
                if not first:
                    store(b - 1)
                if ahead:
                    sp.wait_ge(att_made[NCH - 1], done(b))
                    load_mask(b + 2, k)

            for b in (0, 1):
                step(b, 0, b, b == 0, False)
            with sp.Fori(1, B // 2 - 1) as half:
                for d in range(4):
                    sp.compute_val(half * 2 + d)
                for k in (0, 1):
                    for t, ahead in ((xT_in, 2 + k), (out, k - 1), (maskT_in, 2 + k)):
                        size = int(np.prod(t.shape[1:]))
                        sp.compute_val((half * 2 + ahead) * size)
                        sp.compute_val((half * 2 + ahead) * size * 4)
                for k in (0, 1):
                    step(half * 2 + k, half, k, False, False)
            for b in (B - 2, B - 1):
                step(b, b // 2, b % 2, False, b == B - 1)
            store(B - 1)
            sp.wait_ge(out_stored, 16 * B)

        @block.tensor
        def _(pe):
            def split_matmul(dst, lhs_hi, lhs_lo, rhs_hi, rhs_lo, start, stop):
                nc.tensor.matmul(dst, lhs_hi, rhs_hi, start=start, stop=False)
                nc.tensor.matmul(dst, lhs_hi, rhs_lo, start=False, stop=False)
                return nc.tensor.matmul(dst, lhs_lo, rhs_hi, start=False, stop=stop)

            def weight_matmul(dst, i, rhs_hi, rhs_lo, start, stop):
                return split_matmul(dst, w_hi[:, i, :], w_lo[:, i, :], rhs_hi, rhs_lo, start, stop)

            def weights_ready(i):
                group = next(g for g, (w0, n) in enumerate(GROUPS) if w0 <= i < w0 + n)
                pe.wait_ge(w_lo_made[group], 1)

            def conv1(j, k, again):
                pe.wait_ge(xT_hi_made, done(j))
                pe.wait_ge(xT_lo_made, done(j))
                if again:
                    pe.wait_ge(tanh_z_made, done(j - 2))
                weight_matmul(ps_gate[:, Z, :], W_CONV1, xT_hi[:, k, :], xT_lo[:, k, :], True, True
                              ).then_inc(conv1_done, 1)

            def messages(j, k, again):
                if again:
                    pe.wait_ge(gh_n_made, done(j - 2))
                    pe.wait_ge(cand_in_made, done(j - 2))
                    pe.wait_ge(tanh_r_made, done(j - 2))
                for c in (R, GI, GH, Z):
                    if c == Z:
                        pe.wait_ge(h1_taken, done(j))
                    node = slice(c * P, (c + 1) * P)
                    nc.tensor.matmul(ps_gate[:, c, 0:2 * MC], xT_hi[:, k, node],
                                     wm_split[:, :, :].rearrange("p h m -> p (h m)"), start=True, stop=False)
                    last = nc.tensor.matmul(ps_gate[:, c, 0:MC], xT_lo[:, k, node], wm_split[:, 0, :],
                                            start=False, stop=True)
                last.then_inc(msg_done, 1)

            def turn_rows(j, again):
                pe.wait_ge(rows_made, done(j))
                if again:
                    pe.wait_ge(kern_made[NCH - 1], done(j - 1))
                for c in range(NCH):
                    last = nc.tensor.transpose(ps_dist[:, 0, c * P:(c + 1) * P], rows[:, c, :], ident[:, :])
                last.then_inc(rows_turned, 1)

            def kernel_chunk(b, c, first):
                if c == 0:
                    pe.wait_ge(dist_lhs_made, done(b))
                    pe.wait_ge(dist_rhs_made, done(b))
                if c >= 2:
                    pe.wait_ge(kern_made[c - 2], done(b))
                elif c == 0 and not first:
                    pe.wait_ge(kern_made[NCH - 2], done(b - 1))
                nc.tensor.matmul(ps_dist[:, 1 - c % 2, :], dist_lhs[:, c * P:(c + 1) * P], dist_rhs[:, :],
                                 start=True, stop=True).then_inc(dist_done[c], 1)

            conv_steps = ([(ps_acc[:, 0:RW], W_ODD + j, 1, j, RW) for j in range(ODD)]
                          + [(ps_conv[:, 0:HALF], W_EVEN + j, 0, j, HALF) for j in range(EVEN)]
                          + [(ps_conv[:, HALF:N], W_SUM + j if j else W_EVEN, 2, j, HALF)
                             for j in range(EVEN)])
            OPEN, CLOSE = (0, ODD), (ODD - 1, len(conv_steps) - 1)

            def conv2(b, k, steps, first):
                for t in steps:
                    if first and t == 0:
                        pe.wait_ge(h1_odd_split, 1)
                    if t == (ODD if first else 0):
                        pe.wait_ge(h1_lo_made, done(b))
                        if not first:
                            pe.wait_ge(nmp_lo_made, done(b - 1))
                    if t == ODD and not first:
                        pe.wait_ge(conv_sum_made, done(b - 1))
                    dst, i, phase, j, n = conv_steps[t]
                    if first:
                        weights_ready(i)
                    last = weight_matmul(dst, i, h1_hi[:, k, phase, j:j + n], h1_lo[:, k, phase, j:j + n],
                                         t in OPEN, t in CLOSE)
                    if t == ODD - 1:
                        last.then_inc(conv_r_done, 1)
                    if t == len(conv_steps) - 1:
                        last.then_inc(conv2_done, 1)

            def neighbours(b, k):
                for c in range(NCH):
                    pe.wait_ge(att_lo_made[c], done(b))
                    if c == 0:
                        pe.wait_ge(msg_lo_made, done(b))
                    last = split_matmul(ps_acc[:, :], msg_hi[:, k, c, :], msg_lo[:, k, c, :],
                                        att_hi[:, c, :], att_lo[:, c, :], c == 0, c == NCH - 1)
                last.then_inc(nmp_done, 1)

            def gates(b, k, first, last_batch):
                if not last_batch:
                    pe.wait_ge(msg_sum_made, done(b + 1))
                if first:
                    for i in (W_HH, W_IH_X, W_IH_NMP):
                        weights_ready(i)
                x2 = (xT_hi[:, k, :], xT_lo[:, k, :])
                weight_matmul(ps_gate[:, GH, :], W_HH + 2, *x2, True, True).then_inc(gh_done, 1)
                weight_matmul(ps_gate[:, R, :], W_HH, *x2, True, False)
                if not first:
                    pe.wait_ge(out_made, done(b - 1))
                weight_matmul(ps_gate[:, Z, :], W_HH + 1, *x2, True, False)
                pe.wait_ge(xc_lo_made, done(b))
                xc = (xc_hi[:, :], xc_lo[:, :])
                weight_matmul(ps_gate[:, R, :], W_IH_X, *xc, False, False)
                weight_matmul(ps_gate[:, GI, :], W_IH_X + 2, *xc, True, False)
                weight_matmul(ps_gate[:, Z, :], W_IH_X + 1, *xc, False, False)
                pe.wait_ge(nmp_lo_made, done(b))
                nmp = (nmp_hi[:, :], nmp_lo[:, :])
                weight_matmul(ps_gate[:, R, :], W_IH_NMP, *nmp, False, True).then_inc(r_done, 1)
                weight_matmul(ps_gate[:, GI, :], W_IH_NMP + 2, *nmp, False, True).then_inc(gi_done, 1)
                weight_matmul(ps_gate[:, Z, :], W_IH_NMP + 1, *nmp, False, True).then_inc(z_done, 1)

            def turn_y(j, msg_waits):
                pe.wait_ge(y_made, done(j))
                if msg_waits:
                    pe.wait_ge(msg_sum_made, done(j + 2))
                for c in range(NCH):
                    last = nc.tensor.transpose(ps_gate[:, Z, c * P:(c + 1) * P], y2T[:, c * P:(c + 1) * P], ident[:, :])
                last.then_inc(y_turned, 1)

            pe.wait_ge(warm_zeroed, 1)
            for _ in range(WARM_UP):
                nc.tensor.matmul(ps_conv[:, :], warm_zero[:, 0:P], warm_zero[:, :], start=True, stop=True)
            weights_ready(W_CONV1)
            conv1(0, 0, False)
            pe.wait_ge(wm_lo_made, 1)
            messages(0, 0, False)
            pe.wait_ge(ident_made, 1)

            def step(b, half, k, first, last):
                nk = 1 - k
                if first:
                    conv2(b, k, range(0, 12), first)
                    turn_rows(b, False)
                    conv2(b, k, range(12, 15), first)
                    kernel_chunk(b, 0, first)
                    conv2(b, k, range(15, 17), first)
                    kernel_chunk(b, 1, first)
                    conv2(b, k, range(17, 19), first)
                    kernel_chunk(b, 2, first)
                    conv2(b, k, range(19, 21), first)
                    kernel_chunk(b, 3, first)
                    conv1(b + 1, nk, False)
                    conv2(b, k, range(21, len(conv_steps)), first)
                    messages(b + 1, nk, False)
                else:
                    turn_rows(b, True)
                    conv2(b, k, range(0, 4), first)
                    if not last:
                        conv1(b + 1, nk, True)
                    kernel_chunk(b, 0, first)
                    conv2(b, k, range(4, 6), first)
                    if not last:
                        messages(b + 1, nk, True)
                    kernel_chunk(b, 1, first)
                    conv2(b, k, range(6, 12), first)
                    kernel_chunk(b, 2, first)
                    conv2(b, k, range(12, 14), first)
                    kernel_chunk(b, 3, first)
                    turn_y(b - 1, not last)
                    conv2(b, k, range(14, len(conv_steps)), first)
                pe.wait_ge(odd_part_made, done(b))
                neighbours(b, k)
                gates(b, k, first, last)

            over_batches(pe, step)
            turn_y(B - 1, False)

        @block.scalar
        def _(act):
            def take_x(j, half, k, again):
                act.wait_ge(x_loaded[k], landed(half))
                if again:
                    act.wait_ge(gh_done, done(j - 2))
                    act.wait_ge(r_done, done(j - 2))
                nc.scalar.activation(xT_hi[:, k, :], xT_new[:, k, :], ACT.Copy).then_inc(xT_hi_made, 1)

            def shift_x(j, k, again):
                if not again:
                    act.wait_ge(vec_ready, 1)
                else:
                    act.wait_ge(odd_part_made, done(j - 2))
                nc.scalar.activation(x_shift[:, k, :], xT_new[:, k, :], ACT.Identity, bias=shift_bn[:, 1:2]
                                     ).then_inc(x_shift_made, 1)

            def take_h1(j, again):
                act.wait_ge(conv1_done, done(j))
                if again:
                    act.wait_ge(h1_lo_made, done(j - 1))
                nc.scalar.activation(h1[:, 0:2, :].rearrange("p h u -> p (h u)"), ps_gate[:, Z, :], ACT.Relu,
                                     bias=shift_bn[:, 0:1], scale=scale_bn[:, 0:1]).then_inc(h1_taken, 1)

            def hi_msg(j, k, again):
                act.wait_ge(msg_sum_made, done(j))
                if again:
                    act.wait_ge(nmp_done, done(j - 2))
                nc.scalar.activation(msg_hi[:, k, :, :], msg_sum[:, :, 0:D], ACT.Relu).then_inc(msg_hi_made, 1)

            def lhs(j, again):
                act.wait_ge(rows_turned, done(j))
                if again:
                    act.wait_ge(dist_done[NCH - 1], done(j - 1))
                nc.scalar.activation(dist_lhs[:, :], ps_dist[0:NK, 0, :], ACT.Copy).then_inc(dist_lhs_made, 1)

            def kernel_exp(b, c, first):
                act.wait_ge(dist_done[c], done(b))
                if not first:
                    act.wait_ge(att_made[c], done(b - 1))
                nc.scalar.activation(kern[:, c, :], ps_dist[:, 1 - c % 2, :], ACT.Exp, scale=-1.0).then_inc(kern_made[c], 1)

            def hi_att(b, c, first):
                act.wait_ge(att_made[c], done(b))
                if not first:
                    act.wait_ge(nmp_done, done(b - 1))
                nc.scalar.activation(att_hi[:, c, :], att[:, c, :], ACT.Copy).then_inc(att_hi_made[c], 1)

            def branches(b, first):
                act.wait_ge(conv_sum_made, done(b))
                if not first:
                    act.wait_ge(z_done, done(b - 1))
                nc.scalar.activation(xc_hi[:, :], conv_sum[:, :], ACT.Relu).then_inc(xc_hi_made, 1)
                act.wait_ge(nmp_done, done(b))
                nc.scalar.activation(nmp_hi[:, :], ps_acc[:, :], ACT.Copy).then_inc(nmp_hi_made, 1)
                act.wait_ge(gh_done, done(b))
                if not first:
                    act.wait_ge(reset_made, done(b - 1))
                nc.scalar.activation(gh_n[:, :], ps_gate[:, GH, :], ACT.Identity, bias=vec[:, BHH + 2:BHH + 3]
                                     ).then_inc(gh_n_made, 1)

            def gate_r(j):
                act.wait_ge(r_done, done(j))
                nc.scalar.activation(tanh_r[:, :], ps_gate[:, R, :], ACT.Tanh, bias=half_bias[:, 0:1], scale=0.5
                                     ).then_inc(tanh_r_made, 1)

            def gate_z(j, again):
                act.wait_ge(z_done, done(j))
                if again:
                    act.wait_ge(cand_part_made, done(j - 1))
                nc.scalar.activation(tanh_z[:, :], ps_gate[:, Z, :], ACT.Tanh, bias=half_bias[:, 1:2], scale=0.5
                                     ).then_inc(tanh_z_made, 1)

            def candidate(j, again):
                act.wait_ge(cand_in_made, done(j))
                if again:
                    act.wait_ge(cand_part_made, done(j - 1))
                nc.scalar.activation(cand[:, :], cand_in[:, :], ACT.Tanh, bias=vec[:, BIH + 2:BIH + 3]
                                     ).then_inc(cand_made, 1)

            def hi_weights(g):
                w0, n = GROUPS[g]
                nc.scalar.activation(w_hi[:, w0:w0 + n, :], w_all[:, w0:w0 + n, :], ACT.Copy
                                     ).then_inc(w_hi_made[g], 1)

            take_x(0, 0, 0, False)
            act.wait_ge(wconv1_loaded, 16)
            hi_weights(0)
            act.wait_ge(wmsg_loaded, 16)
            nc.scalar.activation(wm_split[:, 0, :], wm[:, :], ACT.Copy).then_inc(wm_hi_made, 1)
            act.wait_ge(vec_ready, 1)
            take_h1(0, False)
            act.wait_ge(wodd_loaded, 16)
            hi_weights(1)
            hi_weights(2)
            act.wait_ge(weven_loaded, 16)
            hi_weights(3)
            shift_x(0, 0, False)
            hi_weights(4)
            hi_msg(0, 0, False)

            def step(b, half, k, first, last):
                nk = 1 - k
                if not first:
                    gate_r(b - 1)
                if not last:
                    take_x(b + 1, half + k, nk, not first)
                if first:
                    act.wait_ge(wgate_loaded, 16)
                    for g in (7, 8, 9):
                        hi_weights(g)
                    act.wait_ge(wsum_made, 1)
                    hi_weights(5)
                if not first:
                    gate_z(b - 1, not (isinstance(b, int) and b == 1))
                lhs(b, not first)
                if not first:
                    candidate(b - 1, not (isinstance(b, int) and b == 1))
                if not last and not first:
                    take_h1(b + 1, True)
                kernel_exp(b, 0, first)
                if first:
                    act.wait_ge(wsum_made, 2)
                    hi_weights(6)
                kernel_exp(b, 1, first)
                hi_att(b, 0, first)
                if not last:
                    shift_x(b + 1, nk, not first)
                hi_att(b, 1, first)
                kernel_exp(b, 2, first)
                kernel_exp(b, 3, first)
                if first:
                    take_h1(b + 1, True)
                hi_att(b, 2, first)
                hi_att(b, 3, first)
                if not last:
                    hi_msg(b + 1, nk, not first)
                branches(b, first)

            over_batches(act, step, (16, 32))
            gate_r(B - 1)
            gate_z(B - 1, True)
            candidate(B - 1, True)

        @block.vector
        def _(dve):
            def keep_x(j, half, k, again):
                dve.wait_ge(x_loaded[k], landed(half))
                if again:
                    dve.wait_ge(x_part_made, done(j - 2))
                nc.vector.tensor_copy(xT[:, k, :], xT_new[:, k, :]).then_inc(xT_made, 1)

            def sum_h1(j):
                dve.wait_ge(h1_taken, done(j))
                nc.vector.tensor_tensor(h1[:, 2, :], h1[:, 0, :], h1[:, 1, :], ALU.add).then_inc(h1_made, 1)

            def hi_h1(j, k, again):
                if again:
                    dve.wait_ge(conv2_done, done(j - 2))
                dve.wait_ge(h1_made, done(j))
                nc.vector.tensor_copy(h1_hi[:, k, :, PAD:PAD + HALF], h1[:, :, :]).then_inc(h1_hi_made, 1)

            def take_msg(j, again):
                dve.wait_ge(msg_done, done(j))
                nc.vector.tensor_tensor(
                    msg_part[:, :, :], ps_gate[:, :, MC:2 * MC],
                    msg_bias[:, :].rearrange("p (c m) -> p c m", c=1).to_broadcast([P, NCH, MC]), ALU.add
                ).then_inc(msg_part_made, 1)
                if again:
                    dve.wait_ge(msg_lo_made, done(j - 1))
                    dve.wait_ge(rows_made, done(j - 1))
                dve.wait_ge(msg_part_made, done(j))
                nc.vector.tensor_tensor(msg_sum[:, :, :], ps_gate[:, :, 0:MC], msg_part[:, :, :], ALU.add
                                        ).then_inc(msg_sum_made, 1)
                dve.wait_ge(msg_sum_made, done(j))
                if again:
                    dve.wait_ge(rows_turned, done(j - 1))
                nc.vector.tensor_copy(
                    rows[:, :, 0:2 * SE].bitcast(F32R).rearrange("p c (r s) -> p c r s", s=SE),
                    msg_sum[:, :, D:D + SE].rearrange("p c (r s) -> p c r s", r=1).to_broadcast([P, NCH, 2, SE])
                ).then_inc(coord_hi_made, 1)

            def lo_msg(j, k):
                dve.wait_ge(msg_hi_made, done(j))
                nc.vector.scalar_tensor_tensor(
                    out=msg_lo[:, k, :, :], in0=msg_sum[:, :, 0:D], scalar=0.0,
                    in1=msg_hi[:, k, :, :].bitcast(F32), op0=ALU.max, op1=ALU.subtract).then_inc(msg_lo_made, 1)

            def rhs(j, again):
                dve.wait_ge(rows_turned, done(j))
                if again:
                    dve.wait_ge(dist_done[NCH - 1], done(j - 1))
                nc.vector.tensor_copy(dist_rhs[:, :], ps_dist[RHS:RHS + NK, 0, :]).then_inc(dist_rhs_made, 1)

            def mask(b, half, k, c, first):
                if c == 0:
                    dve.wait_ge(mask_loaded[k], landed(half))
                dve.wait_ge(kern_made[c], done(b))
                if not first:
                    dve.wait_ge(att_lo_made[c], done(b - 1))
                nc.vector.tensor_tensor(att[:, c, :], kern[:, c, :], maskT[:, k, c, :], ALU.mult
                                        ).then_inc(att_made[c], 1)

            def take_r(b, k):
                dve.wait_ge(conv_r_done, done(b))
                dve.wait_ge(x_shift_made, done(b))
                nc.vector.scalar_tensor_tensor(out=even_part[:, :], in0=ps_acc[:, 0:HALF],
                                               scalar=scale_bn[:, 1:2], in1=x_shift[:, k, 0:HALF],
                                               op0=ALU.mult, op1=ALU.add)
                nc.vector.scalar_tensor_tensor(out=odd_part[:, :], in0=ps_acc[:, 1:HALF + 1],
                                               scalar=scale_bn[:, 1:2], in1=x_shift[:, k, HALF:N],
                                               op0=ALU.mult, op1=ALU.subtract).then_inc(odd_part_made, 1)

            def lo_last_att(b):
                dve.wait_ge(att_hi_made[NCH - 1], done(b))
                nc.vector.tensor_tensor(att_lo[:, NCH - 1, :], att[:, NCH - 1, :],
                                        att_hi[:, NCH - 1, :].bitcast(F32), ALU.subtract
                                        ).then_inc(att_lo_made[NCH - 1], 1)

            def conv_branch(b, first):
                dve.wait_ge(odd_part_made, done(b))
                dve.wait_ge(conv2_done, done(b))
                nc.vector.scalar_tensor_tensor(out=odd_neg[:, :], in0=ps_conv[:, 0:HALF],
                                               scalar=scale_bn[:, 1:2], in1=odd_part[:, :],
                                               op0=ALU.mult, op1=ALU.add).then_inc(odd_neg_made, 1)
                if not first:
                    dve.wait_ge(xc_lo_made, done(b - 1))
                nc.vector.scalar_tensor_tensor(out=conv_sum[:, 0:HALF], in0=ps_conv[:, 0:HALF],
                                               scalar=scale_bn[:, 1:2], in1=even_part[:, :],
                                               op0=ALU.mult, op1=ALU.add)
                dve.wait_ge(odd_neg_made, done(b))
                nc.vector.scalar_tensor_tensor(out=conv_sum[:, HALF:N], in0=ps_conv[:, HALF:N],
                                               scalar=scale_bn[:, 1:2], in1=odd_neg[:, :],
                                               op0=ALU.mult, op1=ALU.subtract).then_inc(conv_sum_made, 1)

            def lo_branches(b, nk, first, last):
                dve.wait_ge(xc_hi_made, done(b))
                nc.vector.scalar_tensor_tensor(out=xc_lo[:, :], in0=conv_sum[:, :], scalar=0.0,
                                               in1=xc_hi[:, :].bitcast(F32), op0=ALU.max, op1=ALU.subtract
                                               ).then_inc(xc_lo_made, 1)
                if not last:
                    hi_h1(b + 1, nk, not first)
                dve.wait_ge(nmp_hi_made, done(b))
                nc.vector.tensor_tensor(nmp_lo[:, :], ps_acc[:, :], nmp_hi[:, :].bitcast(F32), ALU.subtract
                                        ).then_inc(nmp_lo_made, 1)

            def reset(j):
                dve.wait_ge(gh_n_made, done(j))
                dve.wait_ge(tanh_r_made, done(j))
                nc.vector.scalar_tensor_tensor(out=reset_gh[:, :], in0=tanh_r[:, :], scalar=1.0, in1=gh_n[:, :],
                                               op0=ALU.add, op1=ALU.mult).then_inc(reset_made, 1)
                dve.wait_ge(gi_done, done(j))
                dve.wait_ge(reset_made, done(j))
                nc.vector.scalar_tensor_tensor(out=cand_in[:, :], in0=reset_gh[:, :], scalar=0.5,
                                               in1=ps_gate[:, GI, :], op0=ALU.mult, op1=ALU.add
                                               ).then_inc(cand_in_made, 1)

            def blend_x(j, k):
                dve.wait_ge(tanh_z_made, done(j))
                nc.vector.scalar_tensor_tensor(out=x_part[:, :], in0=tanh_z[:, :], scalar=3.0, in1=xT[:, k, :],
                                               op0=ALU.add, op1=ALU.mult).then_inc(x_part_made, 1)

            def blend_cand(j):
                dve.wait_ge(cand_made, done(j))
                nc.vector.scalar_tensor_tensor(out=cand_part[:, :], in0=tanh_z[:, :], scalar=1.0, in1=cand[:, :],
                                               op0=ALU.subtract, op1=ALU.mult).then_inc(cand_part_made, 1)
                dve.wait_ge(cand_part_made, done(j))
                nc.vector.tensor_tensor(y2T[:, :], x_part[:, :], cand_part[:, :], ALU.subtract
                                        ).then_inc(y_made, 1)

            def statistics(j):
                dve.wait_ge(y_turned, done(j))
                for c in range(NCH):
                    last = nc.vector.bn_stats(stats[:, c, :], ps_gate[:, Z, c * P:(c + 1) * P])
                last.then_inc(stats_made, 1)

            def aggregate(j):
                for c in range(NCH):
                    last = nc.vector.bn_aggr(mean_var[:, c, :], stats[:, c, :])
                last.then_inc(mean_var_made, 1)

            def normalise(j, again):
                dve.wait_ge(rstd_made, done(j))
                if again:
                    dve.wait_ge(out_stored, 16 * j)
                for c in range(NCH):
                    last = nc.vector.tensor_scalar(o_nat[:, c, :], ps_gate[:, Z, c * P:(c + 1) * P],
                                                   mean_var[:, c, 0:1], rstd[:, c:c + 1],
                                                   ALU.subtract, ALU.mult)
                last.then_inc(out_made, 1)

            dve.wait_ge(vec_loaded, 16)
            nc.vector.tensor_scalar(var_eps[:, :], vec[:, V1:V2 + 1:V2 - V1], EPS, None, ALU.add
                                    ).then_inc(setup_dve, 1)
            nc.vector.tensor_tensor(sum_bias[:, :], vec[:, BIH:BIH + 2], vec[:, BHH:BHH + 2], ALU.add
                                    ).then_inc(setup_dve, 1)
            dve.wait_ge(setup_dve, 2)
            nc.vector.tensor_scalar(half_bias[:, :], sum_bias[:, :], 0.5, None, ALU.mult).then_inc(setup_dve, 1)

            def lo_weights(g):
                w0, n = GROUPS[g]
                dve.wait_ge(w_hi_made[g], 1)
                nc.vector.tensor_tensor(w_lo[:, w0:w0 + n, :], w_all[:, w0:w0 + n, :],
                                        w_hi[:, w0:w0 + n, :].bitcast(F32), ALU.subtract).then_inc(w_lo_made[g], 1)

            dve.wait_ge(xT_hi_made, 1)
            nc.vector.tensor_tensor(xT_lo[:, 0, :], xT_new[:, 0, :], xT_hi[:, 0, :].bitcast(F32), ALU.subtract
                                    ).then_inc(xT_lo_made, 1)
            lo_weights(0)
            dve.wait_ge(bn_rstd, 1)
            nc.vector.tensor_tensor(scale_bn[:, :], vec[:, G1:G2 + 1:G2 - G1], rstd_bn[:, :], ALU.mult
                                    ).then_inc(setup_dve, 1)
            dve.wait_ge(setup_dve, 4)
            nc.vector.tensor_tensor(mean_scaled[:, :], vec[:, M1:M2 + 1:M2 - M1], scale_bn[:, :], ALU.mult
                                    ).then_inc(setup_dve, 1)
            dve.wait_ge(setup_dve, 5)
            nc.vector.tensor_tensor(shift_bn[:, :], vec[:, B1:B2 + 1:B2 - B1], mean_scaled[:, :], ALU.subtract
                                    ).then_inc(vec_ready, 1)
            dve.wait_ge(wm_hi_made, 1)
            nc.vector.tensor_tensor(wm_split[:, 1, :], wm[:, :], wm_split[:, 0, :].bitcast(F32), ALU.subtract
                                    ).then_inc(wm_lo_made, 1)
            dve.wait_ge(h1_taken, 1)
            nc.vector.tensor_copy(h1_hi[:, 0, 1, PAD:PAD + HALF], h1[:, 1, :]).then_inc(h1_hi_made, 1)
            dve.wait_ge(h1_hi_made, 1)
            nc.vector.tensor_tensor(h1_lo[:, 0, 1, PAD:PAD + HALF], h1[:, 1, :],
                                    h1_hi[:, 0, 1, PAD:PAD + HALF].bitcast(F32), ALU.subtract
                                    ).then_inc(h1_odd_split, 1)
            lo_weights(1)
            dve.wait_ge(bias_loaded, 16)
            take_msg(0, False)
            nc.vector.tensor_tensor(h1[:, 2, :], h1[:, 0, :], h1[:, 1, :], ALU.add).then_inc(h1_made, 1)
            dve.wait_ge(h1_made, 1)
            nc.vector.tensor_copy(h1_hi[:, 0, 0:3:2, PAD:PAD + HALF], h1[:, 0:3:2, :]).then_inc(h1_hi_even, 1)
            lo_weights(3)
            lo_weights(4)
            lo_msg(0, 0)
            for g in (7, 8, 9):
                lo_weights(g)
            keep_x(0, 0, 0, False)

            def step(b, half, k, first, last):
                nk = 1 - k
                if not first:
                    reset(b - 1)
                rhs(b, not first)
                if first:
                    lo_weights(5)
                if not first:
                    blend_x(b - 1, nk)
                    blend_cand(b - 1)
                mask(b, half, k, 0, first)
                if first:
                    lo_weights(6)
                mask(b, half, k, 1, first)
                if not last and not first:
                    take_msg(b + 1, True)
                take_r(b, k)
                if not first:
                    statistics(b - 1)
                    dve.wait_ge(stats_made, done(b - 1))
                mask(b, half, k, 2, first)
                if not first:
                    aggregate(b - 1)
                mask(b, half, k, 3, first)
                if not last:
                    sum_h1(b + 1)
                lo_last_att(b)
                if first:
                    take_msg(b + 1, True)
                conv_branch(b, first)
                if not first:
                    normalise(b - 1, not (isinstance(b, int) and b == 1))
                lo_branches(b, nk, first, last)
                if not last:
                    lo_msg(b + 1, nk)
                    keep_x(b + 1, half + k, nk, not first)

            over_batches(dve, step, (0, 16, 32))
            reset(B - 1)
            blend_x(B - 1, (B - 1) % 2)
            blend_cand(B - 1)
            statistics(B - 1)
            dve.wait_ge(stats_made, B)
            aggregate(B - 1)
            normalise(B - 1, True)

        @block.gpsimd
        def _(pool):
            def lo_x(j, k):
                pool.wait_ge(xT_hi_made, done(j))
                nc.gpsimd.tensor_tensor(xT_lo[:, k, :], xT_new[:, k, :], xT_hi[:, k, :].bitcast(F32), ALU.subtract
                                        ).then_inc(xT_lo_made, 1)

            def lo_h1(j, k):
                pool.wait_ge(h1_hi_made, done(j))
                nc.gpsimd.tensor_tensor(h1_lo[:, k, :, PAD:PAD + HALF], h1[:, :, :],
                                        h1_hi[:, k, :, PAD:PAD + HALF].bitcast(F32),
                                        ALU.subtract).then_inc(h1_lo_made, 1)

            def lo_att(b, c):
                pool.wait_ge(att_hi_made[c], done(b))
                nc.gpsimd.tensor_tensor(att_lo[:, c, :], att[:, c, :], att_hi[:, c, :].bitcast(F32), ALU.subtract
                                        ).then_inc(att_lo_made[c], 1)

            def make_rows(j):
                hi = rows[:, :, 0:SE]
                lo = rows[:, :, 2 * SE:3 * SE]
                moving = rows[:, :, RHS:RHS + 4 * SE].rearrange("p c (r h s) -> p c r h s", h=2, s=SE)

                def twice(v):
                    return v.rearrange("p c (r s) -> p c r s", r=1).to_broadcast([P, NCH, 2, SE])

                tt = nc.gpsimd.tensor_tensor
                pool.wait_ge(coord_hi_made, done(j))
                coord = msg_sum[:, :, D:D + SE]
                tt(rows[:, :, 2 * SE:4 * SE].rearrange("p c (r s) -> p c r s", s=SE), twice(coord),
                   twice(hi), ALU.subtract)
                tt(coord_sq[:, :, :], coord, coord, ALU.mult)
                m2 = minus_two[:, :].rearrange("p (c r s) -> p c r s", c=1, r=1)
                tt(moving[:, :, :, 0, :], twice(hi), m2.to_broadcast([P, NCH, 2, SE]), ALU.mult
                   ).then_inc(pool_rows, 1)
                pool.wait_ge(pool_rows, 3 * j + 1)
                tt(moving[:, :, :, 1, :], twice(lo), m2.to_broadcast([P, NCH, 2, SE]), ALU.mult)
                tt(norm_part[:, :, :], coord_sq[:, :, 0:1], coord_sq[:, :, 1:2], ALU.add
                   ).then_inc(pool_rows, 1)
                pool.wait_ge(pool_rows, 3 * j + 2)
                both = rows[:, :, SQ:RHS + ONE + 1:RHS + ONE - SQ]
                both_lo = rows[:, :, SQ + 1:RHS + ONE + 2:RHS + ONE - SQ]
                tt(both.bitcast(F32R), norm_part[:, :, :].to_broadcast([P, NCH, 2]),
                   coord_sq[:, :, 2:3].to_broadcast([P, NCH, 2]), ALU.add)
                tt(norm_sq[:, :, :], norm_part[:, :, :], coord_sq[:, :, 2:3], ALU.add).then_inc(pool_rows, 1)
                pool.wait_ge(pool_rows, 3 * j + 3)
                tt(both_lo, norm_sq[:, :, :].to_broadcast([P, NCH, 2]), both, ALU.subtract
                   ).then_inc(rows_made, 1)

            def inverse_std(j, again):
                pool.wait_ge(mean_var_made, done(j))
                if again:
                    pool.wait_ge(out_made, done(j - 1))
                nc.gpsimd.tensor_tensor(var4[:, :], mean_var[:, :, 1], eps4[:, :].to_broadcast([P, NCH]), ALU.add
                                        ).then_inc(var4_made, 1)
                pool.wait_ge(var4_made, done(j))
                nc.gpsimd.tensor_tensor(rstd[:, :], var4[:, :], minus_half[:, :].to_broadcast([P, NCH]), ALU.pow
                                        ).then_inc(rstd_made, 1)

            pool.memset(warm_zero[:, :].bitcast(F32), 0.0).then_inc(warm_zeroed, 1)
            pool.memset(minus_half[:, :], -0.5)
            pool.memset(minus_two[:, :], -2.0)
            pool.memset(eps4[:, :], 4 * EPS).then_inc(consts_made, 1)
            for t in (h1_hi, h1_lo):
                pool.memset(t[:, :, :, 0:PAD].bitcast(F32), 0.0)
                pool.memset(t[:, :, :, PAD + HALF:].bitcast(F32), 0.0)
            pool.memset(rows[:, :, :], 0.0).then_inc(rows_zeroed, 1)
            pool.wait_ge(rows_zeroed, 1)
            pool.memset(rows[:, :, ONE:ONE + 2], 1.0)
            pool.memset(rows[:, :, RHS + SQ:RHS + SQ + 2], 1.0).then_inc(zeros_made, 1)
            pool.memset(ident[:, :], 0.0).then_inc(ident_zero, 1)
            pool.wait_ge(ident_zero, 1)
            pool.affine_select(out=ident[:, :], in_=ident[:, :], compare_op=ALU.not_equal, fill=1.0, base=0,
                               pattern=[[-1, P]], channel_multiplier=1).then_inc(ident_made, 1)
            pool.wait_ge(consts_made, 1)
            pool.wait_ge(setup_dve, 1)
            nc.gpsimd.tensor_tensor(rstd_bn[:, :], var_eps[:, :], minus_half[:, :].to_broadcast([P, 2]), ALU.pow
                                    ).then_inc(bn_rstd, 1)
            pool.wait_ge(w_hi_made[2], 1)
            w0, n = GROUPS[2]
            nc.gpsimd.tensor_tensor(w_lo[:, w0:w0 + n, :], w_all[:, w0:w0 + n, :],
                                    w_hi[:, w0:w0 + n, :].bitcast(F32), ALU.subtract).then_inc(w_lo_made[2], 1)
            make_rows(0)
            pool.wait_ge(h1_hi_even, 1)
            nc.gpsimd.tensor_tensor(h1_lo[:, 0, 0:3:2, PAD:PAD + HALF], h1[:, 0:3:2, :],
                                    h1_hi[:, 0, 0:3:2, PAD:PAD + HALF].bitcast(F32), ALU.subtract
                                    ).then_inc(h1_lo_made, 1)
            pool.wait_ge(wodd_loaded, 16)
            pool.wait_ge(weven_loaded, 16)
            for i in (0, 4):
                nc.gpsimd.tensor_tensor(w_all[:, W_SUM + 1 + i:W_SUM + 5 + i, :],
                                        w_all[:, W_EVEN + 1 + i:W_EVEN + 5 + i, :],
                                        w_all[:, W_ODD + i:W_ODD + 4 + i, :], ALU.add).then_inc(wsum_made, 1)

            def step(b, half, k, first, last):
                nk = 1 - k
                if not last:
                    lo_x(b + 1, nk)
                for c in range(NCH - 1):
                    lo_att(b, c)
                if not first:
                    inverse_std(b - 1, not (isinstance(b, int) and b == 1))
                if not last:
                    make_rows(b + 1)
                    lo_h1(b + 1, nk)

            for b in (0, 1):
                step(b, 0, b, b == 0, False)
            with pool.Fori(1, B // 2 - 1) as half:
                for d in range(4):
                    pool.compute_val(half * 2 + d)
                for d in range(4, 10):
                    pool.compute_val(half * 6 + d)
                for k in (0, 1):
                    step(half * 2 + k, half, k, False, False)
            for b in (B - 2, B - 1):
                step(b, b // 2, b % 2, False, b == B - 1)
            inverse_std(B - 1, True)


def kernel(**inputs):
    import numpy as _np
    import concourse.bacc as _bacc
    from concourse import mybir as _mybir
    from concourse.bass_utils import run_bass_kernel_spmd as _run

    x, adj = _np.asarray(inputs["x"]), _np.asarray(inputs["adj"])
    w = {n[len("L0_gnn_"):]: _np.asarray(a) for n, a in inputs.items() if n.startswith("L0_gnn_")}
    B, N, D = x.shape
    order = _np.concatenate([_np.arange(0, N, 2), _np.arange(1, N, 2)])
    xT = x.transpose(0, 2, 1)[:, :, order]
    maskT = adj.transpose(0, 2, 1)[:, order][:, :, order].reshape(B, N // P, P, N).transpose(0, 2, 1, 3)
    vec = _np.concatenate([w[n].reshape(-1, D) for n in VEC]).T
    conv2 = w["conv2_w"]
    conv = _np.concatenate([w["conv1_w"], conv2[:, :, 1::2], conv2[:, :, 0::2]], axis=2).transpose(1, 2, 0)
    w_ih, w_hh = w["w_ih"].reshape(3, D, 2 * D), w["w_hh"].reshape(3, D, D)
    gate = _np.concatenate([w_ih[:, :, :D], w_ih[:, :, D:], w_hh]).transpose(2, 0, 1)
    msg = _np.concatenate([w["w_msg"], w["w_se"], _np.zeros((1, D), x.dtype)]).T
    msg_bias = _np.concatenate([w["b_msg"], w["b_se"], _np.zeros(1, x.dtype)])
    msg_bias = _np.broadcast_to(msg_bias, (P, len(msg_bias)))
    arrays = {"in_xT": xT, "in_maskT": maskT, "in_vec": vec, "in_conv": conv, "in_gate": gate,
              "in_msg": msg, "in_msg_bias": msg_bias}
    arrays = {name: _np.ascontiguousarray(a) for name, a in arrays.items()}

    nc = _bacc.Bacc("TRN2", target_bir_lowering=False, num_devices=1)
    args = [nc.dram_tensor(name, a.shape, _mybir.dt.from_np(a.dtype), kind="ExternalInput").ap()
            for name, a in arrays.items()]
    out = nc.dram_tensor("out_0_dram", (B, P, N // P, D), _mybir.dt.from_np(x.dtype), kind="ExternalOutput").ap()
    gnn_program(nc, *args, out)
    r = _run(nc, [arrays], core_ids=[0])
    y = r.results[0]["out_0_dram"].transpose(0, 2, 1, 3).reshape(B, N, D)
    return y[:, _np.argsort(order)]
```

```python
from contextlib import ExitStack

import numpy as np
import concourse.bass as bass
from concourse import mybir

F32 = mybir.dt.float32
F32R = mybir.dt.float32r
ALU = mybir.AluOpType
ACT = mybir.ActivationFunctionType

EPS = 1e-5
P = 128
TAPS = 17
WARM_UP = 8
VEC = ["bn1_g", "bn1_b", "bn1_m", "bn1_v", "bn2_g", "bn2_b", "bn2_m", "bn2_v", "b_ih", "b_hh"]
G1, B1, M1, V1, G2, B2, M2, V2, BIH, BHH, NVEC = 0, 1, 2, 3, 4, 5, 6, 7, 8, 11, 14


def gnn_program(nc, xT_in, maskT_in, vec_in, conv_in, gate_in, msg_in, msg_bias_in, out):
    B, D, N = xT_in.shape
    NCH = N // P
    MC = msg_in.shape[1]
    SE = MC - 1 - D
    assert D == P and N == 512 and B % 2 == 0 and B >= 6 and SE == 3
    HALF = N // 2
    EVEN, ODD = (TAPS + 1) // 2, TAPS // 2
    PAD = TAPS // 4
    PHASE = PAD + HALF + PAD + 2
    RW = HALF + 2

    NK = 4 * SE + 4
    SQ, ONE = 4 * SE, 4 * SE + 2
    RHS = 32

    W_CONV1 = 0
    W_ODD = 1
    W_EVEN = W_ODD + ODD
    W_SUM = W_EVEN + EVEN - 1
    W_IH_X = W_SUM + EVEN
    W_IH_NMP, W_HH = W_IH_X + 3, W_IH_X + 6
    NW = W_IH_X + 9
    GROUPS = [(W_CONV1, 1), (W_ODD, 4), (W_ODD + 4, 4), (W_EVEN, 5), (W_EVEN + 5, 4),
              (W_SUM + 1, 4), (W_SUM + 5, 4), (W_HH, 3), (W_IH_X, 3), (W_IH_NMP, 3)]
    W_IN_CONV = W_SUM + 1

    with ExitStack() as ctx:
        def sb(name, shape, dt=F32):
            return ctx.enter_context(nc.sbuf_tensor(name, shape, dt))

        def bank(name, n=1):
            return ctx.enter_context(nc.psum_tensor(name, [P, 512] if n == 1 else [P, n, 512], F32))

        def sem(name):
            return ctx.enter_context(nc.semaphore(name))

        xT_new = sb("xT_new", [P, 2, N])
        maskT = sb("maskT", [P, 2, NCH, N])
        vec = sb("vec", [P, NVEC])
        msg_bias = sb("msg_bias", [P, MC])
        w_all = sb("w_all", [P, NW, P])
        wm = sb("wm", [P, MC])
        warm_zero = sb("warm_zero", [P, N], F32R)
        ident = sb("ident", [P, P])
        minus_half = sb("minus_half", [P, 1])
        minus_two = sb("minus_two", [P, 1])
        var_eps = sb("var_eps", [P, 2])
        rstd_bn = sb("rstd_bn", [P, 2])
        scale_bn = sb("scale_bn", [P, 2])
        shift_bn = sb("shift_bn", [P, 2])
        mean_scaled = sb("mean_scaled", [P, 2])
        half_bias = sb("half_bias", [P, 2])
        sum_bias = sb("sum_bias", [P, 2])
        w_hi = sb("w_hi", [P, NW, P], F32R)
        w_lo = sb("w_lo", [P, NW, P], F32R)
        wm_split = sb("wm_split", [P, 2, MC], F32R)
        xT = sb("xT", [P, 2, N])
        x_shift = sb("x_shift", [P, 2, N])
        xT_hi = sb("xT_hi", [P, 2, N], F32R)
        xT_lo = sb("xT_lo", [P, 2, N], F32R)
        h1 = sb("h1", [P, 3, HALF])
        h1_hi = sb("h1_hi", [P, 2, 3, PHASE], F32R)
        h1_lo = sb("h1_lo", [P, 2, 3, PHASE], F32R)
        msg_hi = sb("msg_hi", [P, 2, NCH, D], F32R)
        msg_lo = sb("msg_lo", [P, 2, NCH, D], F32R)
        msg_part = sb("msg_part", [P, NCH, MC])
        msg_sum = sb("msg_sum", [P, NCH, MC])
        coord_sq = sb("coord_sq", [P, NCH, SE])
        norm_part = sb("norm_part", [P, NCH, 1])
        norm_sq = sb("norm_sq", [P, NCH, 1])
        rows = sb("rows", [P, NCH, P // 2])
        dist_lhs = sb("dist_lhs", [NK, N], F32R)
        dist_rhs = sb("dist_rhs", [NK, N], F32R)
        kern = sb("kern", [P, NCH, N])
        att = sb("att", [P, NCH, N])
        att_hi = sb("att_hi", [P, NCH, N], F32R)
        att_lo = sb("att_lo", [P, NCH, N], F32R)
        even_part = sb("even_part", [P, HALF])
        odd_part = sb("odd_part", [P, HALF])
        odd_neg = sb("odd_neg", [P, HALF])
        conv_sum = sb("conv_sum", [P, N])
        xc_hi = sb("xc_hi", [P, N], F32R)
        xc_lo = sb("xc_lo", [P, N], F32R)
        nmp_hi = sb("nmp_hi", [P, N], F32R)
        nmp_lo = sb("nmp_lo", [P, N], F32R)
        tanh_r = sb("tanh_r", [P, N])
        tanh_z = sb("tanh_z", [P, N])
        gh_n = sb("gh_n", [P, N])
        reset_gh = sb("reset_gh", [P, N])
        cand_in = sb("cand_in", [P, N])
        cand = sb("cand", [P, N])
        x_part = sb("x_part", [P, N])
        cand_part = sb("cand_part", [P, N])
        y2T = sb("y2T", [P, N])
        stats = sb("stats", [P, NCH, 6])
        mean_var = sb("mean_var", [P, NCH, 2])
        var4 = sb("var4", [P, NCH])
        eps4 = sb("eps4", [P, 1])
        rstd = sb("rstd", [P, NCH])
        o_nat = sb("o_nat", [P, NCH, D])

        ps_conv = bank("ps_conv")
        ps_dist = bank("ps_dist", 2)
        ps_acc = bank("ps_acc")
        ps_gate = bank("ps_gate", 4)
        R, Z, GI, GH = 0, 1, 2, 3

        x_loaded = [sem(f"x_loaded{k}") for k in range(2)]
        mask_loaded = [sem(f"mask_loaded{k}") for k in range(2)]
        vec_loaded = sem("vec_loaded")
        bias_loaded = sem("bias_loaded")
        wmsg_loaded = sem("wmsg_loaded")
        wconv1_loaded = sem("wconv1_loaded")
        wodd_loaded = [sem(f"wodd_loaded{i}") for i in range(2)]
        weven_loaded = sem("weven_loaded")
        wgate_loaded = sem("wgate_loaded")
        out_stored = sem("out_stored")
        warm_zeroed = sem("warm_zeroed")
        ident_zero = sem("ident_zero")
        ident_made = sem("ident_made")
        consts_made = sem("consts_made")
        rows_zeroed = sem("rows_zeroed")
        setup_dve = sem("setup_dve")
        bn_rstd = sem("bn_rstd")
        vec_ready = sem("vec_ready")
        wsum_made = sem("wsum_made")
        w_hi_made = [sem(f"w_hi_made{g}") for g in range(len(GROUPS))]
        w_lo_made = [sem(f"w_lo_made{g}") for g in range(len(GROUPS))]
        wm_hi_made = sem("wm_hi_made")
        wm_lo_made = sem("wm_lo_made")
        conv1_done = sem("conv1_done")
        msg_done = sem("msg_done")
        rows_turned = sem("rows_turned")
        dist_done = [sem(f"dist_done{c}") for c in range(NCH)]
        conv_r_done = sem("conv_r_done")
        conv2_done = sem("conv2_done")
        nmp_done = sem("nmp_done")
        gh_done = sem("gh_done")
        r_done = sem("r_done")
        gi_done = sem("gi_done")
        z_done = sem("z_done")
        y_turned = sem("y_turned")
        xT_hi_made = sem("xT_hi_made")
        x_shift_made = sem("x_shift_made")
        h1_taken = sem("h1_taken")
        msg_hi_made = sem("msg_hi_made")
        dist_lhs_made = sem("dist_lhs_made")
        kern_made = [sem(f"kern_made{c}") for c in range(NCH)]
        att_hi_made = [sem(f"att_hi_made{c}") for c in range(NCH)]
        xc_hi_made = sem("xc_hi_made")
        nmp_hi_made = sem("nmp_hi_made")
        gh_n_made = sem("gh_n_made")
        tanh_r_made = sem("tanh_r_made")
        tanh_z_made = sem("tanh_z_made")
        cand_made = sem("cand_made")
        xT_made = sem("xT_made")
        h1_made = sem("h1_made")
        h1_hi_made = sem("h1_hi_made")
        h1_odd_split = sem("h1_odd_split")
        h1_hi_even = sem("h1_hi_even")
        msg_lo_made = sem("msg_lo_made")
        msg_part_made = sem("msg_part_made")
        msg_sum_made = sem("msg_sum_made")
        coord_hi_made = sem("coord_hi_made")
        dist_rhs_made = sem("dist_rhs_made")
        att_made = [sem(f"att_made{c}") for c in range(NCH)]
        odd_part_made = sem("odd_part_made")
        odd_neg_made = sem("odd_neg_made")
        conv_sum_made = sem("conv_sum_made")
        xc_lo_made = sem("xc_lo_made")
        nmp_lo_made = sem("nmp_lo_made")
        reset_made = sem("reset_made")
        cand_in_made = sem("cand_in_made")
        x_part_made = sem("x_part_made")
        cand_part_made = sem("cand_part_made")
        y_made = sem("y_made")
        stats_made = sem("stats_made")
        mean_var_made = sem("mean_var_made")
        out_made = sem("out_made")
        xT_lo_made = sem("xT_lo_made")
        h1_lo_made = sem("h1_lo_made")
        pool_rows = sem("pool_rows")
        rows_made = sem("rows_made")
        att_lo_made = [sem(f"att_lo_made{c}") for c in range(NCH)]
        var4_made = sem("var4_made")
        rstd_made = sem("rstd_made")

        WHOLE = (slice(0, N), range(NCH), ps_gate[:, R, :], ps_gate[:, Z, :], ps_gate[:, GI, :], ps_gate[:, Z, :])
        LAST_HALVES = [
            (slice(0, HALF), range(0, NCH // 2), ps_gate[:, R, 0:HALF], ps_gate[:, Z, 0:HALF],
             ps_gate[:, GI, 0:HALF], ps_acc[:, 0:HALF]),
            (slice(HALF, N), range(NCH // 2, NCH), ps_dist[:, 0, 0:HALF], ps_conv[:, 0:HALF],
             ps_dist[:, 1, 0:HALF], ps_gate[:, R, HALF:N])]

        def done(j):
            return j + 1

        def landed(half):
            return 16 * half + 16

        def over_batches(eng, step, ahead=()):
            for b in (0, 1):
                step(b, 0, b, b == 0, False)
            with eng.Fori(1, B // 2 - 1) as half:
                for d in range(5):
                    eng.compute_val(half * 2 + d)
                for d in ahead:
                    eng.compute_val(half * 16 + d)
                for k in (0, 1):
                    step(half * 2 + k, half, k, False, False)
            for b in (B - 2, B - 1):
                step(b, b // 2, b % 2, False, b == B - 1)

        block = ctx.enter_context(nc.Block())

        @block.sync
        def _(sp):
            def load_x(j, k):
                sp.dma_start(xT_new[:, k], xT_in[bass.ds(j, 1)].rearrange("o p n -> p (o n)")
                             ).then_inc(x_loaded[k], 16)

            def load_mask(j, k):
                sp.dma_start(maskT[:, k], maskT_in[bass.ds(j, 1)].rearrange("o p c n -> p (o c) n")
                             ).then_inc(mask_loaded[k], 16)

            load_x(0, 0)
            sp.dma_start(w_all[:, W_CONV1, :], conv_in[:, W_CONV1, :]).then_inc(wconv1_loaded, 16)
            sp.dma_start(vec[:, :], vec_in).then_inc(vec_loaded, 16)
            sp.dma_start(wm[:, :], msg_in).then_inc(wmsg_loaded, 16)
            for i in (W_ODD, W_ODD + ODD // 2):
                sp.dma_start(w_all[:, i:i + ODD // 2, :], conv_in[:, i:i + ODD // 2, :]
                             ).then_inc(wodd_loaded[i > W_ODD], 16)
            sp.dma_start(msg_bias[:, :], msg_bias_in).then_inc(bias_loaded, 16)
            sp.dma_start(w_all[:, W_EVEN:W_IN_CONV, :], conv_in[:, W_EVEN:W_IN_CONV, :]
                         ).then_inc(weven_loaded, 16)
            load_x(1, 1)
            load_mask(0, 0)
            sp.dma_start(w_all[:, W_IH_X:NW, :], gate_in).then_inc(wgate_loaded, 16)
            load_mask(1, 1)

            def store(j):
                sp.wait_ge(out_made, done(j))
                sp.dma_start(out[bass.ds(j, 1)].rearrange("o p c d -> p (o c) d"), o_nat[:, :, :]
                             ).then_inc(out_stored, 16)

            def step(b, half, k, first, last):
                ahead = not (isinstance(b, int) and b >= B - 2)
                if ahead:
                    sp.wait_ge(xT_lo_made, done(b))
                    sp.wait_ge(x_shift_made, done(b))
                    sp.wait_ge(xT_made, done(b))
                    load_x(b + 2, k)
                if not first:
                    store(b - 1)
                if ahead:
                    sp.wait_ge(att_made[NCH - 1], done(b))
                    load_mask(b + 2, k)

            for b in (0, 1):
                step(b, 0, b, b == 0, False)
            with sp.Fori(1, B // 2 - 1) as half:
                for d in range(4):
                    sp.compute_val(half * 2 + d)
                for k in (0, 1):
                    for t, ahead in ((xT_in, 2 + k), (out, k - 1), (maskT_in, 2 + k)):
                        size = int(np.prod(t.shape[1:]))
                        sp.compute_val((half * 2 + ahead) * size)
                        sp.compute_val((half * 2 + ahead) * size * 4)
                for k in (0, 1):
                    step(half * 2 + k, half, k, False, False)
            for b in (B - 2, B - 1):
                step(b, b // 2, b % 2, False, b == B - 1)
            for h, (_, chunks, *_) in enumerate(LAST_HALVES):
                c = slice(chunks.start, chunks.stop)
                sp.wait_ge(out_made, done(B - 1 + h))
                sp.dma_start(out[B - 1, :, c, :], o_nat[:, c, :]).then_inc(out_stored, 16)
            sp.wait_ge(out_stored, 16 * (B + 1))

        @block.tensor
        def _(pe):
            def split_matmul(dst, lhs_hi, lhs_lo, rhs_hi, rhs_lo, start, stop):
                nc.tensor.matmul(dst, lhs_hi, rhs_hi, start=start, stop=False)
                nc.tensor.matmul(dst, lhs_hi, rhs_lo, start=False, stop=False)
                return nc.tensor.matmul(dst, lhs_lo, rhs_hi, start=False, stop=stop)

            def weight_matmul(dst, i, rhs_hi, rhs_lo, start, stop):
                return split_matmul(dst, w_hi[:, i, :], w_lo[:, i, :], rhs_hi, rhs_lo, start, stop)

            def weights_ready(i):
                group = next(g for g, (w0, n) in enumerate(GROUPS) if w0 <= i < w0 + n)
                pe.wait_ge(w_lo_made[group], 1)

            def conv1(j, k, again):
                pe.wait_ge(xT_lo_made, done(j))
                if again:
                    pe.wait_ge(tanh_z_made, done(j - 2))
                weight_matmul(ps_gate[:, Z, :], W_CONV1, xT_hi[:, k, :], xT_lo[:, k, :], True, True
                              ).then_inc(conv1_done, 1)

            def messages(j, k, again):
                if again:
                    pe.wait_ge(cand_in_made, done(j - 2))
                for c in (R, GI, GH, Z):
                    if c == Z:
                        pe.wait_ge(h1_taken, done(j))
                    node = slice(c * P, (c + 1) * P)
                    nc.tensor.matmul(ps_gate[:, c, 0:2 * MC], xT_hi[:, k, node],
                                     wm_split[:, :, :].rearrange("p h m -> p (h m)"), start=True, stop=False)
                    last = nc.tensor.matmul(ps_gate[:, c, 0:MC], xT_lo[:, k, node], wm_split[:, 0, :],
                                            start=False, stop=True)
                last.then_inc(msg_done, 1)

            def turn_rows(j):
                pe.wait_ge(rows_made, done(j))
                for g in range(NCH // 2):
                    last = nc.tensor.transpose(ps_dist[:, 0, g * P:(g + 1) * P],
                                               rows[:, 2 * g:2 * g + 2, :].rearrange("p c r -> p (c r)"), ident[:, :])
                last.then_inc(rows_turned, 1)

            def kernel_chunk(b, c):
                if c == 0:
                    pe.wait_ge(dist_lhs_made, done(b))
                    pe.wait_ge(dist_rhs_made, done(b))
                if c >= 2:
                    pe.wait_ge(kern_made[c - 2], done(b))
                nc.tensor.matmul(ps_dist[:, 1 - c % 2, :], dist_lhs[:, c * P:(c + 1) * P], dist_rhs[:, :],
                                 start=True, stop=True).then_inc(dist_done[c], 1)

            conv_steps = ([(ps_acc[:, 0:RW], W_ODD + j, 1, j, RW) for j in range(ODD)]
                          + [(ps_conv[:, 0:HALF], W_EVEN + j, 0, j, HALF) for j in range(EVEN)]
                          + [(ps_conv[:, HALF:N], W_SUM + j if j else W_EVEN, 2, j, HALF)
                             for j in range(EVEN)])
            OPEN, CLOSE = (0, ODD), (ODD - 1, len(conv_steps) - 1)

            def conv2(b, k, steps, first):
                for t in steps:
                    if first and t == 0:
                        pe.wait_ge(h1_odd_split, 1)
                    if t == (ODD if first else 0):
                        pe.wait_ge(h1_lo_made, done(b))
                    dst, i, phase, j, n = conv_steps[t]
                    if first:
                        weights_ready(i)
                    last = weight_matmul(dst, i, h1_hi[:, k, phase, j:j + n], h1_lo[:, k, phase, j:j + n],
                                         t in OPEN, t in CLOSE)
                    if t == ODD - 1:
                        last.then_inc(conv_r_done, 1)
                    if t == len(conv_steps) - 1:
                        last.then_inc(conv2_done, 1)

            def neighbours(b, k):
                for c in range(NCH):
                    pe.wait_ge(att_lo_made[c], done(b))
                    if c == 0:
                        pe.wait_ge(msg_lo_made, done(b))
                    last = split_matmul(ps_acc[:, :], msg_hi[:, k, c, :], msg_lo[:, k, c, :],
                                        att_hi[:, c, :], att_lo[:, c, :], c == 0, c == NCH - 1)
                last.then_inc(nmp_done, 1)

            def gates(b, k, first):
                pe.wait_ge(msg_sum_made, done(b + 1))
                if first:
                    for i in (W_HH, W_IH_X, W_IH_NMP):
                        weights_ready(i)
                x2 = (xT_hi[:, k, :], xT_lo[:, k, :])
                weight_matmul(ps_gate[:, GH, :], W_HH + 2, *x2, True, True).then_inc(gh_done, 1)
                weight_matmul(ps_gate[:, R, :], W_HH, *x2, True, False)
                if not first:
                    pe.wait_ge(out_made, done(b - 1))
                weight_matmul(ps_gate[:, Z, :], W_HH + 1, *x2, True, False)
                pe.wait_ge(xc_lo_made, done(b))
                xc = (xc_hi[:, :], xc_lo[:, :])
                weight_matmul(ps_gate[:, R, :], W_IH_X, *xc, False, False)
                weight_matmul(ps_gate[:, GI, :], W_IH_X + 2, *xc, True, False)
                weight_matmul(ps_gate[:, Z, :], W_IH_X + 1, *xc, False, False)
                pe.wait_ge(nmp_lo_made, done(b))
                nmp = (nmp_hi[:, :], nmp_lo[:, :])
                weight_matmul(ps_gate[:, R, :], W_IH_NMP, *nmp, False, True).then_inc(r_done, 1)
                weight_matmul(ps_gate[:, GI, :], W_IH_NMP + 2, *nmp, False, True).then_inc(gi_done, 1)
                weight_matmul(ps_gate[:, Z, :], W_IH_NMP + 1, *nmp, False, True).then_inc(z_done, 1)

            def last_gates(k):
                b = B - 1
                x2 = (xT_hi[:, k, :], xT_lo[:, k, :])
                weight_matmul(ps_gate[:, GH, :], W_HH + 2, *x2, True, True).then_inc(gh_done, 1)
                pe.wait_ge(kern_made[NCH - 1], done(b))
                pe.wait_ge(conv_sum_made, done(b))
                pe.wait_ge(out_made, done(b - 1))
                for nodes, _, ps_r, ps_z, _, _ in LAST_HALVES:
                    x2 = (xT_hi[:, k, nodes], xT_lo[:, k, nodes])
                    weight_matmul(ps_r, W_HH, *x2, True, False)
                    weight_matmul(ps_z, W_HH + 1, *x2, True, False)
                pe.wait_ge(xc_lo_made, done(b))
                for nodes, _, ps_r, ps_z, ps_gi, _ in LAST_HALVES:
                    xc = (xc_hi[:, nodes], xc_lo[:, nodes])
                    weight_matmul(ps_r, W_IH_X, *xc, False, False)
                    weight_matmul(ps_gi, W_IH_X + 2, *xc, True, False)
                    weight_matmul(ps_z, W_IH_X + 1, *xc, False, False)
                    if nodes.start == 0:
                        pe.wait_ge(nmp_lo_made, done(b))
                    nmp = (nmp_hi[:, nodes], nmp_lo[:, nodes])
                    weight_matmul(ps_r, W_IH_NMP, *nmp, False, True).then_inc(r_done, 1)
                    weight_matmul(ps_gi, W_IH_NMP + 2, *nmp, False, True).then_inc(gi_done, 1)
                    weight_matmul(ps_z, W_IH_NMP + 1, *nmp, False, True).then_inc(z_done, 1)

            def turn_y(j, msg_waits, part=WHOLE):
                if msg_waits:
                    pe.wait_ge(msg_sum_made, done(j + 2))
                else:
                    pe.wait_ge(y_made, done(j))
                nodes, chunks, *_, dst = part
                for i, c in enumerate(chunks):
                    last = nc.tensor.transpose(dst[:, i * P:(i + 1) * P], y2T[:, c * P:(c + 1) * P], ident[:, :])
                last.then_inc(y_turned, 1)

            pe.wait_ge(warm_zeroed, 1)
            for _ in range(WARM_UP):
                nc.tensor.matmul(ps_conv[:, :], warm_zero[:, 0:P], warm_zero[:, :], start=True, stop=True)
            weights_ready(W_CONV1)
            conv1(0, 0, False)
            pe.wait_ge(wm_lo_made, 1)
            messages(0, 0, False)
            pe.wait_ge(ident_made, 1)

            def step(b, half, k, first, last):
                nk = 1 - k
                if first:
                    conv2(b, k, range(0, 12), first)
                    turn_rows(b)
                    conv2(b, k, range(12, 15), first)
                    kernel_chunk(b, 0)
                    conv2(b, k, range(15, 17), first)
                    kernel_chunk(b, 1)
                    conv2(b, k, range(17, 19), first)
                    kernel_chunk(b, 2)
                    conv1(b + 1, nk, False)
                    conv2(b, k, range(19, 21), first)
                    kernel_chunk(b, 3)
                    conv2(b, k, range(21, 23), first)
                    messages(b + 1, nk, False)
                    conv2(b, k, range(23, len(conv_steps)), first)
                else:
                    turn_rows(b)
                    conv2(b, k, range(0, 4), first)
                    if not last:
                        conv1(b + 1, nk, True)
                    kernel_chunk(b, 0)
                    conv2(b, k, range(4, 6), first)
                    if not last:
                        messages(b + 1, nk, True)
                    kernel_chunk(b, 1)
                    conv2(b, k, range(6, 12), first)
                    kernel_chunk(b, 2)
                    conv2(b, k, range(12, 14), first)
                    kernel_chunk(b, 3)
                    turn_y(b - 1, not last)
                    conv2(b, k, range(14, len(conv_steps)), first)
                pe.wait_ge(odd_part_made, done(b))
                neighbours(b, k)
                if last:
                    last_gates(k)
                else:
                    gates(b, k, first)

            over_batches(pe, step)
            for h in range(2):
                turn_y(B - 1 + h, False, LAST_HALVES[h])

        @block.scalar
        def _(act):
            def take_x(j, half, k, again):
                act.wait_ge(x_loaded[k], landed(half))
                if again:
                    act.wait_ge(gh_done, done(j - 2))
                    act.wait_ge(r_done, done(j - 2))
                nc.scalar.activation(xT_hi[:, k, :], xT_new[:, k, :], ACT.Copy).then_inc(xT_hi_made, 1)

            def shift_x(j, k, again):
                if not again:
                    act.wait_ge(vec_ready, 1)
                else:
                    act.wait_ge(odd_part_made, done(j - 2))
                nc.scalar.activation(x_shift[:, k, :], xT_new[:, k, :], ACT.Identity, bias=shift_bn[:, 1:2]
                                     ).then_inc(x_shift_made, 1)

            def take_h1(j, again):
                act.wait_ge(conv1_done, done(j))
                if again:
                    act.wait_ge(h1_lo_made, done(j - 1))
                nc.scalar.activation(h1[:, 0:2, :].rearrange("p h u -> p (h u)"), ps_gate[:, Z, :], ACT.Relu,
                                     bias=shift_bn[:, 0:1], scale=scale_bn[:, 0:1]).then_inc(h1_taken, 1)

            def hi_msg(j, k, again):
                act.wait_ge(msg_sum_made, done(j))
                if again:
                    act.wait_ge(nmp_done, done(j - 2))
                nc.scalar.activation(msg_hi[:, k, :, :], msg_sum[:, :, 0:D], ACT.Relu).then_inc(msg_hi_made, 1)

            def lhs(j, again):
                act.wait_ge(rows_turned, done(j))
                if again:
                    act.wait_ge(dist_done[NCH - 1], done(j - 1))
                for i in range(2):
                    last = nc.scalar.activation(
                        dist_lhs[:, :].rearrange("r (g i n) -> r g i n", i=2, n=P)[:, :, i, :],
                        ps_dist[i * P // 2:i * P // 2 + NK, 0, 0:N // 2].rearrange("r (g n) -> r g n", n=P), ACT.Copy)
                last.then_inc(dist_lhs_made, 1)

            def kernel_exp(b, c, first):
                act.wait_ge(dist_done[c], done(b))
                if not first:
                    act.wait_ge(att_made[c], done(b - 1))
                nc.scalar.activation(kern[:, c, :], ps_dist[:, 1 - c % 2, :], ACT.Exp, scale=-1.0
                                     ).then_inc(kern_made[c], 1)

            def hi_att(b, c, first):
                act.wait_ge(att_made[c], done(b))
                if not first:
                    act.wait_ge(nmp_done, done(b - 1))
                nc.scalar.activation(att_hi[:, c, :], att[:, c, :], ACT.Copy).then_inc(att_hi_made[c], 1)

            def branches(b, first):
                act.wait_ge(conv_sum_made, done(b))
                if not first:
                    act.wait_ge(z_done, done(b - 1))
                nc.scalar.activation(xc_hi[:, :], conv_sum[:, :], ACT.Relu).then_inc(xc_hi_made, 1)
                act.wait_ge(nmp_done, done(b))
                nc.scalar.activation(nmp_hi[:, :], ps_acc[:, :], ACT.Copy).then_inc(nmp_hi_made, 1)
                act.wait_ge(gh_done, done(b))
                if not first:
                    act.wait_ge(reset_made, done(b - 1))
                nc.scalar.activation(gh_n[:, :], ps_gate[:, GH, :], ACT.Identity, bias=vec[:, BHH + 2:BHH + 3]
                                     ).then_inc(gh_n_made, 1)

            def gate_r(j, part=WHOLE):
                nodes, _, ps_r, *_ = part
                act.wait_ge(r_done, done(j))
                nc.scalar.activation(tanh_r[:, nodes], ps_r, ACT.Tanh, bias=half_bias[:, 0:1], scale=0.5
                                     ).then_inc(tanh_r_made, 1)

            def gate_z(j, again, part=WHOLE):
                nodes, _, _, ps_z, *_ = part
                act.wait_ge(z_done, done(j))
                if again:
                    act.wait_ge(cand_part_made, done(j - 1))
                nc.scalar.activation(tanh_z[:, nodes], ps_z, ACT.Tanh, bias=half_bias[:, 1:2], scale=0.5
                                     ).then_inc(tanh_z_made, 1)

            def candidate(j, again, part=WHOLE):
                nodes = part[0]
                act.wait_ge(cand_in_made, done(j))
                if again:
                    act.wait_ge(cand_part_made, done(j - 1))
                nc.scalar.activation(cand[:, nodes], cand_in[:, nodes], ACT.Tanh, bias=vec[:, BIH + 2:BIH + 3]
                                     ).then_inc(cand_made, 1)

            def hi_weights(g):
                w0, n = GROUPS[g]
                nc.scalar.activation(w_hi[:, w0:w0 + n, :], w_all[:, w0:w0 + n, :], ACT.Copy
                                     ).then_inc(w_hi_made[g], 1)

            take_x(0, 0, 0, False)
            act.wait_ge(wconv1_loaded, 16)
            hi_weights(0)
            act.wait_ge(wmsg_loaded, 16)
            nc.scalar.activation(wm_split[:, 0, :], wm[:, :], ACT.Copy).then_inc(wm_hi_made, 1)
            act.wait_ge(wodd_loaded[0], 16)
            hi_weights(1)
            act.wait_ge(vec_ready, 1)
            take_h1(0, False)
            act.wait_ge(wodd_loaded[1], 16)
            hi_weights(2)
            act.wait_ge(weven_loaded, 16)
            hi_weights(3)
            shift_x(0, 0, False)
            hi_weights(4)
            hi_msg(0, 0, False)

            def step(b, half, k, first, last):
                nk = 1 - k
                if not first:
                    gate_r(b - 1)
                if not last:
                    take_x(b + 1, half + k, nk, not first)
                if not first:
                    gate_z(b - 1, not (isinstance(b, int) and b == 1))
                lhs(b, not first)
                if first:
                    act.wait_ge(wsum_made, 1)
                    hi_weights(5)
                if not first:
                    candidate(b - 1, not (isinstance(b, int) and b == 1))
                if not last and not first:
                    take_h1(b + 1, True)
                kernel_exp(b, 0, first)
                if first:
                    act.wait_ge(wsum_made, 2)
                    hi_weights(6)
                kernel_exp(b, 1, first)
                hi_att(b, 0, first)
                if not last:
                    shift_x(b + 1, nk, not first)
                hi_att(b, 1, first)
                kernel_exp(b, 2, first)
                if first:
                    take_h1(b + 1, True)
                kernel_exp(b, 3, first)
                hi_att(b, 2, first)
                hi_att(b, 3, first)
                if first:
                    act.wait_ge(wgate_loaded, 16)
                    for g in (7, 8, 9):
                        hi_weights(g)
                if not last:
                    hi_msg(b + 1, nk, not first)
                branches(b, first)

            over_batches(act, step, (16, 32))
            gate_r(B - 1, LAST_HALVES[0])
            gate_z(B - 1, True, LAST_HALVES[0])
            candidate(B - 1, True, LAST_HALVES[0])
            gate_r(B, LAST_HALVES[1])
            gate_z(B, False, LAST_HALVES[1])
            candidate(B, False, LAST_HALVES[1])

        @block.vector
        def _(dve):
            def keep_x(j, half, k, again):
                dve.wait_ge(x_loaded[k], landed(half))
                if again:
                    dve.wait_ge(x_part_made, done(j - 2))
                nc.vector.tensor_copy(xT[:, k, :], xT_new[:, k, :]).then_inc(xT_made, 1)

            def sum_h1(j):
                dve.wait_ge(h1_taken, done(j))
                nc.vector.tensor_tensor(h1[:, 2, :], h1[:, 0, :], h1[:, 1, :], ALU.add).then_inc(h1_made, 1)

            def hi_h1(j, k, again):
                if again:
                    dve.wait_ge(conv2_done, done(j - 2))
                dve.wait_ge(h1_made, done(j))
                nc.vector.tensor_copy(h1_hi[:, k, :, PAD:PAD + HALF], h1[:, :, :]).then_inc(h1_hi_made, 1)

            def take_msg(j, again):
                dve.wait_ge(msg_done, done(j))
                nc.vector.tensor_tensor(
                    msg_part[:, :, :], ps_gate[:, :, MC:2 * MC],
                    msg_bias[:, :].rearrange("p (c m) -> p c m", c=1).to_broadcast([P, NCH, MC]), ALU.add
                ).then_inc(msg_part_made, 1)
                if again:
                    dve.wait_ge(msg_lo_made, done(j - 1))
                    dve.wait_ge(rows_made, done(j - 1))
                dve.wait_ge(msg_part_made, done(j))
                nc.vector.tensor_tensor(msg_sum[:, :, :], ps_gate[:, :, 0:MC], msg_part[:, :, :], ALU.add
                                        ).then_inc(msg_sum_made, 1)
                dve.wait_ge(msg_sum_made, done(j))
                if again:
                    dve.wait_ge(rows_turned, done(j - 1))
                nc.vector.tensor_copy(
                    rows[:, :, 0:2 * SE].bitcast(F32R).rearrange("p c (r s) -> p c r s", s=SE),
                    msg_sum[:, :, D:D + SE].rearrange("p c (r s) -> p c r s", r=1).to_broadcast([P, NCH, 2, SE])
                ).then_inc(coord_hi_made, 1)

            def lo_msg(j, k):
                dve.wait_ge(msg_hi_made, done(j))
                nc.vector.scalar_tensor_tensor(
                    out=msg_lo[:, k, :, :], in0=msg_sum[:, :, 0:D], scalar=0.0,
                    in1=msg_hi[:, k, :, :].bitcast(F32), op0=ALU.max, op1=ALU.subtract).then_inc(msg_lo_made, 1)

            def rhs(j, again):
                dve.wait_ge(rows_turned, done(j))
                if again:
                    dve.wait_ge(dist_done[NCH - 1], done(j - 1))
                for i in range(2):
                    row = i * P // 2 + RHS
                    last = nc.vector.tensor_copy(
                        dist_rhs[:, :].rearrange("r (g i n) -> r g i n", i=2, n=P)[:, :, i, :],
                        ps_dist[row:row + NK, 0, 0:N // 2].rearrange("r (g n) -> r g n", n=P))
                last.then_inc(dist_rhs_made, 1)

            def mask(b, half, k, c, first):
                if c == 0:
                    dve.wait_ge(mask_loaded[k], landed(half))
                dve.wait_ge(kern_made[c], done(b))
                if not first:
                    dve.wait_ge(att_lo_made[c], done(b - 1))
                nc.vector.tensor_tensor(att[:, c, :], kern[:, c, :], maskT[:, k, c, :], ALU.mult
                                        ).then_inc(att_made[c], 1)

            def take_r(b, k):
                dve.wait_ge(conv_r_done, done(b))
                dve.wait_ge(x_shift_made, done(b))
                nc.vector.scalar_tensor_tensor(out=even_part[:, :], in0=ps_acc[:, 0:HALF],
                                               scalar=scale_bn[:, 1:2], in1=x_shift[:, k, 0:HALF],
                                               op0=ALU.mult, op1=ALU.add)
                nc.vector.scalar_tensor_tensor(out=odd_part[:, :], in0=ps_acc[:, 1:HALF + 1],
                                               scalar=scale_bn[:, 1:2], in1=x_shift[:, k, HALF:N],
                                               op0=ALU.mult, op1=ALU.subtract).then_inc(odd_part_made, 1)

            def lo_last_att(b):
                dve.wait_ge(att_hi_made[NCH - 1], done(b))
                nc.vector.tensor_tensor(att_lo[:, NCH - 1, :], att[:, NCH - 1, :],
                                        att_hi[:, NCH - 1, :].bitcast(F32), ALU.subtract
                                        ).then_inc(att_lo_made[NCH - 1], 1)

            def conv_branch(b, first):
                dve.wait_ge(odd_part_made, done(b))
                dve.wait_ge(conv2_done, done(b))
                nc.vector.scalar_tensor_tensor(out=odd_neg[:, :], in0=ps_conv[:, 0:HALF],
                                               scalar=scale_bn[:, 1:2], in1=odd_part[:, :],
                                               op0=ALU.mult, op1=ALU.add).then_inc(odd_neg_made, 1)
                if not first:
                    dve.wait_ge(xc_lo_made, done(b - 1))
                nc.vector.scalar_tensor_tensor(out=conv_sum[:, 0:HALF], in0=ps_conv[:, 0:HALF],
                                               scalar=scale_bn[:, 1:2], in1=even_part[:, :],
                                               op0=ALU.mult, op1=ALU.add)
                dve.wait_ge(odd_neg_made, done(b))
                nc.vector.scalar_tensor_tensor(out=conv_sum[:, HALF:N], in0=ps_conv[:, HALF:N],
                                               scalar=scale_bn[:, 1:2], in1=odd_neg[:, :],
                                               op0=ALU.mult, op1=ALU.subtract).then_inc(conv_sum_made, 1)

            def lo_branches(b, nk, first, last):
                dve.wait_ge(xc_hi_made, done(b))
                nc.vector.scalar_tensor_tensor(out=xc_lo[:, :], in0=conv_sum[:, :], scalar=0.0,
                                               in1=xc_hi[:, :].bitcast(F32), op0=ALU.max, op1=ALU.subtract
                                               ).then_inc(xc_lo_made, 1)
                if not last:
                    hi_h1(b + 1, nk, not first)
                dve.wait_ge(nmp_hi_made, done(b))
                nc.vector.tensor_tensor(nmp_lo[:, :], ps_acc[:, :], nmp_hi[:, :].bitcast(F32), ALU.subtract
                                        ).then_inc(nmp_lo_made, 1)

            def reset(j, part=WHOLE):
                nodes, _, _, _, ps_gi, _ = part
                if part is not LAST_HALVES[1]:
                    dve.wait_ge(gh_n_made, done(j))
                dve.wait_ge(tanh_r_made, done(j))
                nc.vector.scalar_tensor_tensor(out=reset_gh[:, nodes], in0=tanh_r[:, nodes], scalar=1.0,
                                               in1=gh_n[:, nodes], op0=ALU.add, op1=ALU.mult
                                               ).then_inc(reset_made, 1)
                dve.wait_ge(gi_done, done(j))
                dve.wait_ge(reset_made, done(j))
                nc.vector.scalar_tensor_tensor(out=cand_in[:, nodes], in0=reset_gh[:, nodes], scalar=0.5,
                                               in1=ps_gi, op0=ALU.mult, op1=ALU.add
                                               ).then_inc(cand_in_made, 1)

            def blend_x(j, k, part=WHOLE):
                nodes = part[0]
                dve.wait_ge(tanh_z_made, done(j))
                nc.vector.scalar_tensor_tensor(out=x_part[:, nodes], in0=tanh_z[:, nodes], scalar=3.0,
                                               in1=xT[:, k, nodes], op0=ALU.add, op1=ALU.mult
                                               ).then_inc(x_part_made, 1)

            def blend_cand(j, part=WHOLE):
                nodes = part[0]
                dve.wait_ge(cand_made, done(j))
                nc.vector.scalar_tensor_tensor(out=cand_part[:, nodes], in0=tanh_z[:, nodes], scalar=1.0,
                                               in1=cand[:, nodes], op0=ALU.subtract, op1=ALU.mult
                                               ).then_inc(cand_part_made, 1)
                dve.wait_ge(cand_part_made, done(j))
                nc.vector.tensor_tensor(y2T[:, nodes], x_part[:, nodes], cand_part[:, nodes], ALU.subtract
                                        ).then_inc(y_made, 1)

            def statistics(j, part=WHOLE):
                _, chunks, *_, src = part
                dve.wait_ge(y_turned, done(j))
                for i, c in enumerate(chunks):
                    last = nc.vector.bn_stats(stats[:, c, :], src[:, i * P:(i + 1) * P])
                last.then_inc(stats_made, 1)

            def aggregate(chunks=range(NCH)):
                for c in chunks:
                    last = nc.vector.bn_aggr(mean_var[:, c, :], stats[:, c, :])
                last.then_inc(mean_var_made, 1)

            def normalise(j, again, part=WHOLE):
                _, chunks, *_, src = part
                dve.wait_ge(rstd_made, done(j))
                if again:
                    dve.wait_ge(out_stored, 16 * j)
                for i, c in enumerate(chunks):
                    last = nc.vector.tensor_scalar(o_nat[:, c, :], src[:, i * P:(i + 1) * P],
                                                   mean_var[:, c, 0:1], rstd[:, c:c + 1],
                                                   ALU.subtract, ALU.mult)
                last.then_inc(out_made, 1)

            dve.wait_ge(vec_loaded, 16)
            nc.vector.tensor_scalar(var_eps[:, :], vec[:, V1:V2 + 1:V2 - V1], EPS, None, ALU.add
                                    ).then_inc(setup_dve, 1)
            nc.vector.tensor_tensor(sum_bias[:, :], vec[:, BIH:BIH + 2], vec[:, BHH:BHH + 2], ALU.add
                                    ).then_inc(setup_dve, 1)
            dve.wait_ge(setup_dve, 2)
            nc.vector.tensor_scalar(half_bias[:, :], sum_bias[:, :], 0.5, None, ALU.mult).then_inc(setup_dve, 1)

            def lo_weights(g):
                w0, n = GROUPS[g]
                dve.wait_ge(w_hi_made[g], 1)
                nc.vector.tensor_tensor(w_lo[:, w0:w0 + n, :], w_all[:, w0:w0 + n, :],
                                        w_hi[:, w0:w0 + n, :].bitcast(F32), ALU.subtract).then_inc(w_lo_made[g], 1)

            dve.wait_ge(xT_hi_made, 1)
            nc.vector.tensor_tensor(xT_lo[:, 0, :], xT_new[:, 0, :], xT_hi[:, 0, :].bitcast(F32), ALU.subtract
                                    ).then_inc(xT_lo_made, 1)
            lo_weights(0)
            dve.wait_ge(bn_rstd, 1)
            nc.vector.tensor_tensor(scale_bn[:, :], vec[:, G1:G2 + 1:G2 - G1], rstd_bn[:, :], ALU.mult
                                    ).then_inc(setup_dve, 1)
            dve.wait_ge(setup_dve, 4)
            nc.vector.tensor_tensor(mean_scaled[:, :], vec[:, M1:M2 + 1:M2 - M1], scale_bn[:, :], ALU.mult
                                    ).then_inc(setup_dve, 1)
            dve.wait_ge(setup_dve, 5)
            nc.vector.tensor_tensor(shift_bn[:, :], vec[:, B1:B2 + 1:B2 - B1], mean_scaled[:, :], ALU.subtract
                                    ).then_inc(vec_ready, 1)
            dve.wait_ge(wm_hi_made, 1)
            nc.vector.tensor_tensor(wm_split[:, 1, :], wm[:, :], wm_split[:, 0, :].bitcast(F32), ALU.subtract
                                    ).then_inc(wm_lo_made, 1)
            lo_weights(1)
            dve.wait_ge(h1_taken, 1)
            nc.vector.tensor_copy(h1_hi[:, 0, 1, PAD:PAD + HALF], h1[:, 1, :]).then_inc(h1_hi_made, 1)
            dve.wait_ge(h1_hi_made, 1)
            nc.vector.tensor_tensor(h1_lo[:, 0, 1, PAD:PAD + HALF], h1[:, 1, :],
                                    h1_hi[:, 0, 1, PAD:PAD + HALF].bitcast(F32), ALU.subtract
                                    ).then_inc(h1_odd_split, 1)
            sum_h1(0)
            dve.wait_ge(h1_made, 1)
            nc.vector.tensor_copy(h1_hi[:, 0, 0:3:2, PAD:PAD + HALF], h1[:, 0:3:2, :]).then_inc(h1_hi_even, 1)
            dve.wait_ge(bias_loaded, 16)
            take_msg(0, False)
            lo_weights(3)
            lo_weights(4)
            lo_msg(0, 0)

            def step(b, half, k, first, last):
                nk = 1 - k
                if not first:
                    reset(b - 1)
                rhs(b, not first)
                if first:
                    lo_weights(5)
                if not first:
                    blend_x(b - 1, nk)
                    blend_cand(b - 1)
                mask(b, half, k, 0, first)
                if first:
                    lo_weights(6)
                mask(b, half, k, 1, first)
                if not last and not first:
                    take_msg(b + 1, True)
                take_r(b, k)
                if first:
                    keep_x(0, 0, 0, False)
                if not first:
                    statistics(b - 1)
                    dve.wait_ge(stats_made, done(b - 1))
                mask(b, half, k, 2, first)
                if not first:
                    aggregate()
                mask(b, half, k, 3, first)
                if not last:
                    sum_h1(b + 1)
                lo_last_att(b)
                if first:
                    take_msg(b + 1, True)
                    lo_weights(7)
                conv_branch(b, first)
                if not first:
                    normalise(b - 1, not (isinstance(b, int) and b == 1))
                lo_branches(b, nk, first, last)
                if not last:
                    lo_msg(b + 1, nk)
                    keep_x(b + 1, half + k, nk, not first)

            over_batches(dve, step, (0, 16, 32))
            reset(B - 1, LAST_HALVES[0])
            blend_x(B - 1, (B - 1) % 2, LAST_HALVES[0])
            reset(B, LAST_HALVES[1])
            blend_cand(B - 1, LAST_HALVES[0])
            blend_x(B, (B - 1) % 2, LAST_HALVES[1])
            blend_cand(B, LAST_HALVES[1])
            for h, part in enumerate(LAST_HALVES):
                statistics(B - 1 + h, part)
                dve.wait_ge(stats_made, done(B - 1 + h))
                aggregate(part[1])
            for h, part in enumerate(LAST_HALVES):
                normalise(B - 1 + h, h == 0, part)

        @block.gpsimd
        def _(pool):
            def lo_x(j, k):
                pool.wait_ge(xT_hi_made, done(j))
                nc.gpsimd.tensor_tensor(xT_lo[:, k, :], xT_new[:, k, :], xT_hi[:, k, :].bitcast(F32), ALU.subtract
                                        ).then_inc(xT_lo_made, 1)

            def lo_h1(j, k):
                pool.wait_ge(h1_hi_made, done(j))
                nc.gpsimd.tensor_tensor(h1_lo[:, k, :, PAD:PAD + HALF], h1[:, :, :],
                                        h1_hi[:, k, :, PAD:PAD + HALF].bitcast(F32),
                                        ALU.subtract).then_inc(h1_lo_made, 1)

            def lo_att(b, c):
                pool.wait_ge(att_hi_made[c], done(b))
                nc.gpsimd.tensor_tensor(att_lo[:, c, :], att[:, c, :], att_hi[:, c, :].bitcast(F32), ALU.subtract
                                        ).then_inc(att_lo_made[c], 1)

            def make_rows(j):
                hi = rows[:, :, 0:SE]
                lo = rows[:, :, 2 * SE:3 * SE]
                moving = rows[:, :, RHS:RHS + 4 * SE].rearrange("p c (r h s) -> p c r h s", h=2, s=SE)

                def twice(v):
                    return v.rearrange("p c (r s) -> p c r s", r=1).to_broadcast([P, NCH, 2, SE])

                tt = nc.gpsimd.tensor_tensor
                pool.wait_ge(coord_hi_made, done(j))
                coord = msg_sum[:, :, D:D + SE]
                tt(rows[:, :, 2 * SE:4 * SE].rearrange("p c (r s) -> p c r s", s=SE), twice(coord),
                   twice(hi), ALU.subtract)
                tt(coord_sq[:, :, :], coord, coord, ALU.mult)
                m2 = minus_two[:, :].rearrange("p (c r s) -> p c r s", c=1, r=1)
                tt(moving[:, :, :, 0, :], twice(hi), m2.to_broadcast([P, NCH, 2, SE]), ALU.mult
                   ).then_inc(pool_rows, 1)
                pool.wait_ge(pool_rows, 3 * j + 1)
                tt(moving[:, :, :, 1, :], twice(lo), m2.to_broadcast([P, NCH, 2, SE]), ALU.mult)
                tt(norm_part[:, :, :], coord_sq[:, :, 0:1], coord_sq[:, :, 1:2], ALU.add
                   ).then_inc(pool_rows, 1)
                pool.wait_ge(pool_rows, 3 * j + 2)
                both = rows[:, :, SQ:RHS + ONE + 1:RHS + ONE - SQ]
                both_lo = rows[:, :, SQ + 1:RHS + ONE + 2:RHS + ONE - SQ]
                tt(both.bitcast(F32R), norm_part[:, :, :].to_broadcast([P, NCH, 2]),
                   coord_sq[:, :, 2:3].to_broadcast([P, NCH, 2]), ALU.add)
                tt(norm_sq[:, :, :], norm_part[:, :, :], coord_sq[:, :, 2:3], ALU.add).then_inc(pool_rows, 1)
                pool.wait_ge(pool_rows, 3 * j + 3)
                tt(both_lo, norm_sq[:, :, :].to_broadcast([P, NCH, 2]), both, ALU.subtract
                   ).then_inc(rows_made, 1)

            def inverse_std(j, again, c=slice(0, NCH)):
                n = c.stop - c.start
                pool.wait_ge(mean_var_made, done(j))
                if again:
                    pool.wait_ge(out_made, done(j - 1))
                nc.gpsimd.tensor_tensor(var4[:, c], mean_var[:, c, 1], eps4[:, :].to_broadcast([P, n]), ALU.add
                                        ).then_inc(var4_made, 1)
                pool.wait_ge(var4_made, done(j))
                nc.gpsimd.tensor_tensor(rstd[:, c], var4[:, c], minus_half[:, :].to_broadcast([P, n]), ALU.pow
                                        ).then_inc(rstd_made, 1)

            pool.memset(warm_zero[:, :].bitcast(F32), 0.0).then_inc(warm_zeroed, 1)
            pool.memset(minus_half[:, :], -0.5)
            pool.memset(minus_two[:, :], -2.0)
            pool.memset(eps4[:, :], 4 * EPS).then_inc(consts_made, 1)
            for t in (h1_hi, h1_lo):
                pool.memset(t[:, :, :, 0:PAD].bitcast(F32), 0.0)
                pool.memset(t[:, :, :, PAD + HALF:].bitcast(F32), 0.0)
            pool.memset(rows[:, :, :], 0.0).then_inc(rows_zeroed, 1)
            pool.wait_ge(rows_zeroed, 1)
            pool.memset(rows[:, :, ONE:ONE + 2], 1.0)
            pool.memset(rows[:, :, RHS + SQ:RHS + SQ + 2], 1.0)
            pool.memset(ident[:, :], 0.0).then_inc(ident_zero, 1)
            pool.wait_ge(ident_zero, 1)
            pool.affine_select(out=ident[:, :], in_=ident[:, :], compare_op=ALU.not_equal, fill=1.0, base=0,
                               pattern=[[-1, P]], channel_multiplier=1).then_inc(ident_made, 1)
            pool.wait_ge(consts_made, 1)
            pool.wait_ge(setup_dve, 1)
            nc.gpsimd.tensor_tensor(rstd_bn[:, :], var_eps[:, :], minus_half[:, :].to_broadcast([P, 2]), ALU.pow
                                    ).then_inc(bn_rstd, 1)

            def lo_weights(g):
                w0, n = GROUPS[g]
                pool.wait_ge(w_hi_made[g], 1)
                nc.gpsimd.tensor_tensor(w_lo[:, w0:w0 + n, :], w_all[:, w0:w0 + n, :],
                                        w_hi[:, w0:w0 + n, :].bitcast(F32), ALU.subtract).then_inc(w_lo_made[g], 1)

            lo_weights(2)
            pool.wait_ge(h1_hi_even, 1)
            nc.gpsimd.tensor_tensor(h1_lo[:, 0, 0:3:2, PAD:PAD + HALF], h1[:, 0:3:2, :],
                                    h1_hi[:, 0, 0:3:2, PAD:PAD + HALF].bitcast(F32), ALU.subtract
                                    ).then_inc(h1_lo_made, 1)
            make_rows(0)
            pool.wait_ge(wodd_loaded[0], 16)
            pool.wait_ge(wodd_loaded[1], 16)
            pool.wait_ge(weven_loaded, 16)
            for i in (0, 4):
                nc.gpsimd.tensor_tensor(w_all[:, W_SUM + 1 + i:W_SUM + 5 + i, :],
                                        w_all[:, W_EVEN + 1 + i:W_EVEN + 5 + i, :],
                                        w_all[:, W_ODD + i:W_ODD + 4 + i, :], ALU.add).then_inc(wsum_made, 1)

            def step(b, half, k, first, last):
                nk = 1 - k
                if not last:
                    lo_x(b + 1, nk)
                for c in range(NCH - 1):
                    lo_att(b, c)
                if first:
                    lo_weights(8)
                    lo_weights(9)
                else:
                    inverse_std(b - 1, not (isinstance(b, int) and b == 1))
                if not last:
                    make_rows(b + 1)
                    lo_h1(b + 1, nk)

            for b in (0, 1):
                step(b, 0, b, b == 0, False)
            with pool.Fori(1, B // 2 - 1) as half:
                for d in range(4):
                    pool.compute_val(half * 2 + d)
                for d in range(4, 10):
                    pool.compute_val(half * 6 + d)
                for k in (0, 1):
                    step(half * 2 + k, half, k, False, False)
            for b in (B - 2, B - 1):
                step(b, b // 2, b % 2, False, b == B - 1)
            inverse_std(B - 1, True, slice(0, NCH // 2))
            inverse_std(B, False, slice(NCH // 2, NCH))


def kernel(**inputs):
    import numpy as _np
    import concourse.bacc as _bacc
    from concourse import mybir as _mybir
    from concourse.bass_utils import run_bass_kernel_spmd as _run

    x, adj = _np.asarray(inputs["x"]), _np.asarray(inputs["adj"])
    w = {n[len("L0_gnn_"):]: _np.asarray(a) for n, a in inputs.items() if n.startswith("L0_gnn_")}
    B, N, D = x.shape
    order = _np.concatenate([_np.arange(0, N, 2), _np.arange(1, N, 2)])
    xT = x.transpose(0, 2, 1)[:, :, order]
    maskT = adj.transpose(0, 2, 1)[:, order][:, :, order].reshape(B, N // P, P, N).transpose(0, 2, 1, 3)
    vec = _np.concatenate([w[n].reshape(-1, D) for n in VEC]).T
    conv2 = w["conv2_w"]
    conv = _np.concatenate([w["conv1_w"], conv2[:, :, 1::2], conv2[:, :, 0::2]], axis=2).transpose(1, 2, 0)
    w_ih, w_hh = w["w_ih"].reshape(3, D, 2 * D), w["w_hh"].reshape(3, D, D)
    gate = _np.concatenate([w_ih[:, :, :D], w_ih[:, :, D:], w_hh]).transpose(2, 0, 1)
    msg = _np.concatenate([w["w_msg"], w["w_se"], _np.zeros((1, D), x.dtype)]).T
    msg_bias = _np.concatenate([w["b_msg"], w["b_se"], _np.zeros(1, x.dtype)])
    msg_bias = _np.broadcast_to(msg_bias, (P, len(msg_bias)))
    arrays = {"in_xT": xT, "in_maskT": maskT, "in_vec": vec, "in_conv": conv, "in_gate": gate,
              "in_msg": msg, "in_msg_bias": msg_bias}
    arrays = {name: _np.ascontiguousarray(a) for name, a in arrays.items()}

    nc = _bacc.Bacc("TRN2", target_bir_lowering=False, num_devices=1)
    args = [nc.dram_tensor(name, a.shape, _mybir.dt.from_np(a.dtype), kind="ExternalInput").ap()
            for name, a in arrays.items()]
    out = nc.dram_tensor("out_0_dram", (B, P, N // P, D), _mybir.dt.from_np(x.dtype), kind="ExternalOutput").ap()
    gnn_program(nc, *args, out)
    r = _run(nc, [arrays], core_ids=[0])
    y = r.results[0]["out_0_dram"].transpose(0, 2, 1, 3).reshape(B, N, D)
    return y[:, _np.argsort(order)]
```
